# Optimizing a Trainium2 kernel written in Bass

```python
import numpy as np
import jax
import jax.numpy as jnp

def _softmax(x, axis=-1):
    return jax.nn.softmax(x, axis=axis)

def _gelu(x):
    return jax.nn.gelu(x, approximate=True)

def _silu(x):
    return jax.nn.silu(x)

def _sigmoid(x):
    return jax.nn.sigmoid(x)

def _layernorm(x, axis=-1, eps=1e-05):
    m = jnp.mean(x, axis=axis, keepdims=True)
    v = jnp.var(x, axis=axis, keepdims=True)
    return (x - m) / jnp.sqrt(v + eps)

def _scatter_add(tgt, idx, src, axis=0):
    return tgt.at[idx].add(src)

def _segment_sum(src, seg, n):
    return jax.ops.segment_sum(src, seg, n)
kernel_name = 'mk_rec_standalone_d1_rec_r8_e3acd2'

def setup_inputs(seed: int=0):
    np.random.seed(seed)
    _w = jnp.asarray

    def _rec_inputs():
        import jax
        import jax.numpy as jnp
        _rk = jax.random.key(seed)
        r_x0 = -0.000292821 + 1.00034 * jax.random.normal(jax.random.fold_in(_rk, 1), (512, 32, 64), jnp.float32)
        return r_x0
    r_x0 = _rec_inputs()

    def _L0_rec_setup():
        import jax, jax.numpy as jnp
        import numpy as np
        BATCH, FIELD, EMB = (256, 32, 64)
        LAYER_SIZES = [64, 64, 64]
        OUT_DIM = 1
        FINAL_DIM = sum(LAYER_SIZES)

        def _cin_layer(W, b, xk, x0):
            return jnp.einsum('ohm,bhd,bmd->bod', W, xk, x0) + b[None, :, None]
        key = jax.random.key(seed)
        ks = jax.random.split(key, 10)
        inp = {'x0': jax.random.normal(ks[0], (BATCH, FIELD, EMB), dtype=jnp.float32), 'W1': jax.random.normal(ks[1], (LAYER_SIZES[0], FIELD, FIELD), dtype=jnp.float32) * 0.05, 'b1': jax.random.normal(ks[2], (LAYER_SIZES[0],), dtype=jnp.float32) * 0.05, 'W2': jax.random.normal(ks[3], (LAYER_SIZES[1], LAYER_SIZES[0], FIELD), dtype=jnp.float32) * 0.05, 'b2': jax.random.normal(ks[4], (LAYER_SIZES[1],), dtype=jnp.float32) * 0.05, 'W3': jax.random.normal(ks[5], (LAYER_SIZES[2], LAYER_SIZES[1], FIELD), dtype=jnp.float32) * 0.05, 'b3': jax.random.normal(ks[6], (LAYER_SIZES[2],), dtype=jnp.float32) * 0.05, 'W_out': jax.random.normal(ks[7], (FINAL_DIM, OUT_DIM), dtype=jnp.float32) * 0.05, 'b_out': jax.random.normal(ks[8], (OUT_DIM,), dtype=jnp.float32) * 0.05}
        return inp
    _L0_rec_all = _L0_rec_setup()
    _L0_rec_in = {k: v for k, v in _L0_rec_all.items() if k in ('W1', 'b1', 'W2', 'b2', 'W3', 'b3', 'W_out', 'b_out')}
    del _L0_rec_all
    return {'r_x0': r_x0, 'L0_rec_W1': _L0_rec_in['W1'], 'L0_rec_b1': _L0_rec_in['b1'], 'L0_rec_W2': _L0_rec_in['W2'], 'L0_rec_b2': _L0_rec_in['b2'], 'L0_rec_W3': _L0_rec_in['W3'], 'L0_rec_b3': _L0_rec_in['b3'], 'L0_rec_W_out': _L0_rec_in['W_out'], 'L0_rec_b_out': _L0_rec_in['b_out']}

def reference(r_x0, L0_rec_W1, L0_rec_b1, L0_rec_W2, L0_rec_b2, L0_rec_W3, L0_rec_b3, L0_rec_W_out, L0_rec_b_out):
    import jax
    import jax.numpy as jnp

    def _L0_rec_ref(x0, W1, b1, W2, b2, W3, b3, W_out, b_out):
        import jax, jax.numpy as jnp
        import numpy as np
        BATCH, FIELD, EMB = (256, 32, 64)
        LAYER_SIZES = [64, 64, 64]
        OUT_DIM = 1
        FINAL_DIM = sum(LAYER_SIZES)

        def _cin_layer(W, b, xk, x0):
            return jnp.einsum('ohm,bhd,bmd->bod', W, xk, x0) + b[None, :, None]
        h1 = _cin_layer(W1, b1, x0, x0)
        h2 = _cin_layer(W2, b2, h1, x0)
        h3 = _cin_layer(W3, b3, h2, x0)
        stacked = jnp.concatenate([h1, h2, h3], axis=1)
        pooled = stacked.sum(axis=2)
        return pooled @ W_out + b_out
    y = _L0_rec_ref(r_x0, L0_rec_W1, L0_rec_b1, L0_rec_W2, L0_rec_b2, L0_rec_W3, L0_rec_b3, L0_rec_W_out, L0_rec_b_out)
    return y

_drawn_inputs = setup_inputs


def setup_inputs(seed=0):
    import zlib

    import numpy as np

    out = dict(_drawn_inputs(seed))
    spreads = {}
    factors = {'L0_rec_b2': 6.441}
    for name, (base, spread) in spreads.items():
        noise = np.random.default_rng([zlib.crc32(name.encode()), seed]).standard_normal(out[name].shape)
        drawn = base * np.exp(spread * noise) if base else spread * noise
        out[name] = jnp.asarray(drawn.astype(out[name].dtype))
    for name, factor in factors.items():
        out[name] = (out[name] * factor).astype(out[name].dtype)
    return out
```

```python
from contextlib import ExitStack

import numpy as np

import concourse.bass as bass
from concourse import mybir

F32 = mybir.dt.float32
F32R = mybir.dt.float32r
ALU = mybir.AluOpType
ACT = mybir.ActivationFunctionType
AX_X = mybir.AxisListType.X

P = 128
FIELDS = 32
UNITS = 64
QUADS = P // FIELDS
SHIFT_TILES = 4
SPLIT = 3
BANK = 512


def constants():
    eye = np.eye(P, dtype=np.float32)
    row, col = np.arange(P)[:, None], np.arange(P)[None, :]
    rolls = [
        (row < 2 * FIELDS) & (row % FIELDS == (col % FIELDS + QUADS * t + col // FIELDS + 1) % FIELDS)
        for t in range(SHIFT_TILES)
    ]
    g = np.arange(QUADS)[None, :]
    half = row // UNITS
    picks = [(g // 2 == s) & (g % 2 == half) for s in range(2)] + [row // FIELDS == g]
    return eye, np.concatenate(rolls, 1).astype(np.float32), np.concatenate(picks, 1).astype(np.float32)


def build(nc, x, W1, b1, W2, b2, W3, b3, W_out, b_out, eye_in, rolls_in, picks_in, y):
    BATCH, _, EMB = x.shape
    BJ = 16
    COLS = BJ * EMB
    HALVES = COLS // BANK
    GRANULES = BATCH // (QUADS * BJ)
    CHUNKS = GRANULES * QUADS
    MM = FIELDS * FIELDS
    HOM = UNITS * FIELDS
    KINDS = 4

    with ExitStack() as ctx:
        def sb(name, shape, dt=F32):
            return ctx.enter_context(nc.sbuf_tensor(name, shape, dt))

        def sem(name):
            return ctx.enter_context(nc.semaphore(name))

        acc = ctx.enter_context(nc.psum_tensor("acc", [P, 4, BANK], F32))
        rolled = ctx.enter_context(nc.psum_tensor("rolled", [P, 4, BANK], F32))

        x_all = sb("x_all", [P, GRANULES * COLS])
        x_rep = sb("x_rep", [P, QUADS, COLS])
        parts = sb("parts", [P, KINDS, COLS], F32R)
        x_sq = sb("x_sq", [P, COLS])
        stack = sb("stack", [P, QUADS, COLS], F32R)
        z = sb("z", [P, 2, SHIFT_TILES, COLS])
        z_hi = sb("z_hi", [P, 2, SPLIT, COLS], F32R)
        z_lo = sb("z_lo", [P, 2, SPLIT, COLS], F32R)
        q_sb = sb("q_sb", [P, 2, COLS])
        hq = sb("hq", [P, 2, COLS])
        hq_sum = sb("hq_sum", [P, 2, GRANULES * BJ])
        x_sum = sb("x_sum", [P, GRANULES * BJ])

        eye = sb("eye", [P, P])
        rolls_f = sb("rolls_f", [P, SHIFT_TILES, P])
        rolls = sb("rolls", [P, SHIFT_TILES, P], F32R)
        picks = sb("picks", [P, 3, QUADS])
        cols = sb("cols", [P, 8])
        v_w2 = sb("v_w2", [UNITS, FIELDS + 1])
        v_rep = sb("v_rep", [UNITS, QUADS, FIELDS])
        sym = sb("sym", [P, 4 * SHIFT_TILES, FIELDS])
        low = sb("low", [P, KINDS, FIELDS])
        w_hi = sb("w_hi", [P, SPLIT, P], F32R)
        w_lo = sb("w_lo", [P, SPLIT, P], F32R)
        w_full = sb("w_full", [P, SHIFT_TILES - SPLIT, P]) if SPLIT < SHIFT_TILES else None
        low_hi = sb("low_hi", [P, P], F32R)
        low_lo = sb("low_lo", [P, P], F32R)
        beta = sb("beta", [P, 1])
        beta_pick = sb("beta_pick", [P, QUADS])
        b23 = sb("b23", [P, P])
        w23 = sb("w23", [P, QUADS])
        y_sb = sb("y_sb", [P, QUADS])

        w2_sb = z[0:UNITS, 0, 0:2, :].rearrange("p a b -> p (a b)")
        w3_sb = z[0:UNITS, 0, 2:4, :].rearrange("p a b -> p (a b)")
        DIAG = 2 * FIELDS + 1
        wg = sb("wg", [P, FIELDS * DIAG])
        wgt = z[:, 1, :, :].rearrange("p a b -> p (a b)")[:, 0:FIELDS * DIAG]

        def rows64(t):
            return t[:, 0:2 * MM].rearrange("p (m c) -> p m c", c=2 * FIELDS)

        def diagonals(t):
            return t.rearrange("p (m c) -> p c m", c=DIAG)

        w3_in, w2_in, w1_in, consts_in = sem("w3_in"), sem("w2_in"), sem("w1_in"), sem("consts_in")
        cols_in, cols_late_in, rolls_read, low_zero = sem("cols_in"), sem("cols_late_in"), sem("rolls_in"), sem("low_zero")
        v_done, v_copied, g_done, g_copied = sem("v_done"), sem("v_copied"), sem("g_done"), sem("g_copied")
        wg_doubled, wgt_done, sym_done, low_done = sem("wg_doubled"), sem("wgt_done"), sem("sym_done"), sem("low_done")
        turned, hi_done, weights_ready, rolls_ready = sem("turned"), sem("hi_done"), sem("weights_ready"), sem("rolls_ready")
        x_in = sem("x_in")
        x_hi_done, x_lo_done = sem("x_hi_done"), sem("x_lo_done")
        sq_done, sq_hi_done, sq_lo_done = sem("sq_done"), sem("sq_hi_done"), sem("sq_lo_done")
        stack_in = [sem(f"stack_in{g}") for g in range(QUADS)]
        rep_in = [sem(f"rep_in{g}") for g in range(QUADS)]
        roll_done, z_done, hi_ready, lo_ready, z_used = (
            sem("roll_done"), sem("z_done"), sem("hi_ready"), sem("lo_ready"), sem("z_used"))
        stack_used, q_ready, hq_done, summed, x_summed = (
            sem("stack_used"), sem("q_ready"), sem("hq_done"), sem("summed"), sem("x_summed"))
        beta_done, beta_ready, tail_ready, y_done, y_ready, y_out = (
            sem("beta_done"), sem("beta_ready"), sem("tail_ready"), sem("y_done"), sem("y_ready"), sem("y_out"))

        def over_granules(engine, body):
            body(0, True, False)
            with engine.Fori(1, GRANULES - 1) as G:
                body(G, False, False)
            body(GRANULES - 1, False, True)

        def x_cols(G):
            return x_all[:, bass.ds(G * COLS, COLS)]

        block = ctx.enter_context(nc.Block())

        @block.sync
        def _(sp):
            x_dram = x.rearrange("(G j g) m d -> G (g m) j d", j=BJ, g=QUADS)

            def load_x(G):
                sp.dma_start(x_cols(G).rearrange("p (j d) -> p j d", d=EMB),
                             x_dram[bass.ds(G, 1)].rearrange("o p j d -> (o p) j d")).then_inc(x_in, 16)

            load_x(0)
            sp.dma_start(eye[:], eye_in).then_inc(consts_in, 16)
            sp.dma_start(rolls_f[:].rearrange("p t c -> p (t c)"), rolls_in).then_inc(rolls_read, 16)

            def granule(G, first, last):
                sp.wait_ge(x_in, 16 * G + 16)
                for g in range(QUADS):
                    if not first:
                        sp.wait_ge(z_done, SHIFT_TILES * (QUADS * (G - 1) + g + 1))
                    for k in range(QUADS):
                        sp.dma_start(x_rep[FIELDS * k:FIELDS * (k + 1), g, :],
                                     x_all[FIELDS * g:FIELDS * (g + 1), bass.ds(G * COLS, COLS)]).then_inc(rep_in[g], 16)
                    if not first:
                        sp.wait_ge(stack_used, QUADS * (G - 1) + g + 1)
                        sp.nop(nofuse=True)
                    for k, ready in enumerate((x_hi_done, x_lo_done, sq_hi_done, sq_lo_done)):
                        if g == 0:
                            sp.wait_ge(ready, G + 1)
                        sp.dma_start(stack[FIELDS * k:FIELDS * (k + 1), g, :].bitcast(F32),
                                     parts[FIELDS * g:FIELDS * (g + 1), k, :].bitcast(F32)).then_inc(stack_in[g], 16)
                    if g == 0 and not last:
                        load_x(G + 1)

            over_granules(sp, granule)
            sp.wait_ge(y_ready, 1)
            sp.dma_start(y.rearrange("(p g) o -> p (g o)", g=QUADS), y_sb[:]).then_inc(y_out, 16)
            sp.wait_ge(y_out, 16)

        @block.gpsimd
        def _(pool):
            pool.dma_start(picks[:].rearrange("p a b -> p (a b)"), picks_in).then_inc(cols_late_in, 16)
            pool.dma_start(cols[0:UNITS, 3:4], b2.rearrange("(p o) -> p o", o=1)).then_inc(cols_late_in, 16)
            pool.dma_start(cols[UNITS:P, 3:4], b3.rearrange("(p o) -> p o", o=1)).then_inc(cols_late_in, 16)
            pool.dma_start(cols[:, 4:5], W_out[UNITS:3 * UNITS, :]).then_inc(cols_late_in, 16)
            pool.dma_start(cols[:, 5:6], b_out.rearrange("(p o) -> p o", o=1).to_broadcast((P, 1))).then_inc(cols_late_in, 16)
            pool.dma_start(cols[0:UNITS, 0:1], b1.rearrange("(p o) -> p o", o=1)).then_inc(cols_late_in, 16)
            pool.dma_start(cols[UNITS:P, 0:1], W_out[0:UNITS, :]).then_inc(cols_late_in, 16)

            def lows(c, s, first):
                for t in range(SPLIT):
                    pool.wait_ge(hi_ready, SPLIT * c + t + 1)
                    if not first:
                        pool.wait_ge(z_used, SHIFT_TILES * (c - 2) + t + 1)
                    nc.gpsimd.tensor_tensor(z_lo[:, s, t, :], z[:, s, t, :], z_hi[:, s, t, :].bitcast(F32),
                                            ALU.subtract).then_inc(lo_ready, 1)

            def granule(G, first, last):
                for g in range(QUADS):
                    lows(QUADS * G + g, g % 2, first and g < 2)

            over_granules(pool, granule)

        @block.scalar
        def _(act):
            act.dma_start(w3_sb, W3.rearrange("o h m -> o (h m)")).then_inc(w3_in, 16)
            act.dma_start(cols[0:UNITS, 1:2], W_out[UNITS:2 * UNITS, :]).then_inc(cols_in, 16)
            act.dma_start(cols[0:UNITS, 2:3], W_out[2 * UNITS:3 * UNITS, :]).then_inc(cols_in, 16)
            act.dma_start(w2_sb, W2.rearrange("o h m -> o (h m)")).then_inc(w2_in, 16)
            act.dma_start(rows64(wg)[0:UNITS, :, 0:FIELDS], W1).then_inc(w1_in, 16)

            def pre(G, first):
                act.wait_ge(x_in, 16 * G + 16)
                if not first:
                    for g in range(QUADS):
                        act.wait_ge(stack_in[g], 16 * KINDS * G)
                act.nop(nofuse=True)
                nc.scalar.activation(parts[:, 0, :], x_cols(G), ACT.Copy).then_inc(x_hi_done, 1)
                if not first:
                    act.wait_ge(sq_lo_done, G)
                act.nop(nofuse=True)
                nc.scalar.activation(x_sq[:], x_cols(G), ACT.Square).then_inc(sq_done, 1)

            def highs(c, s, t, first):
                act.wait_ge(z_done, SHIFT_TILES * c + t + 1)
                if not first:
                    act.wait_ge(z_used, SHIFT_TILES * (c - 2) + t + 1)
                nc.scalar.activation(z_hi[:, s, t, :], z[:, s, t, :], ACT.Copy).then_inc(hi_ready, 1)

            def q_out(c, s, first):
                act.wait_ge(z_used, SHIFT_TILES * (c + 1))
                if not first:
                    act.wait_ge(hq_done, c - 1)
                nc.scalar.activation(q_sb[0:UNITS, s, :], acc[UNITS:P, 2 * s:2 * s + 2, :].rearrange("p a b -> p (a b)"),
                                     ACT.Identity, bias=cols[UNITS:P, 0:1]).then_inc(q_ready, 1)

            pre(0, True)
            act.wait_ge(g_done, 1)
            g_psum = acc[UNITS:P, :, 0:8 * (FIELDS + 1)].rearrange("p a (b c) -> p a b c", c=FIELDS + 1)
            nc.scalar.activation(rows64(wg)[UNITS:P, :, 0:FIELDS].rearrange("p (a b) c -> p a b c", a=4),
                                 g_psum[:, :, :, 0:FIELDS], ACT.Copy).then_inc(g_copied, 1)
            act.wait_ge(g_copied, 1)
            act.wait_ge(w1_in, 16)
            nc.scalar.activation(rows64(wgt)[:, :, FIELDS:FIELDS + FIELDS // 2],
                                 rows64(wg)[:, 0:FIELDS // 2, 0:FIELDS].rearrange("p r m -> p m r"),
                                 ACT.Copy).then_inc(wgt_done, 1)
            act.wait_ge(turned, 2)
            nc.scalar.activation(w_hi[:].rearrange("p t c -> p (t c)"), acc[:, 0, 0:SPLIT * P], ACT.Copy).then_inc(hi_done, 1)
            nc.scalar.activation(low_hi[:], acc[:, 1, 0:P], ACT.Copy).then_inc(hi_done, 1)
            act.wait_ge(cols_late_in, 7 * 16)
            for t in range(SPLIT):
                highs(0, 0, t, True)

            def granule(G, first, last):
                for g in range(QUADS):
                    c = QUADS * G + g
                    if not (first and g == 0):
                        q_out(c - 1, (g + 1) % 2, first and g < 3)
                    if not (last and g == QUADS - 1):
                        for t in range(SPLIT):
                            highs(c + 1, (g + 1) % 2, t, first and g == 0)
                    if g == 0 and not last:
                        pre(G + 1, False)

            over_granules(act, granule)
            q_out(CHUNKS - 1, 1, False)

        @block.vector
        def _(dve):
            def x_low(G):
                dve.wait_ge(x_hi_done, G + 1)
                nc.vector.tensor_tensor(parts[:, 1, :], x_cols(G), parts[:, 0, :].bitcast(F32),
                                        ALU.subtract).then_inc(x_lo_done, 1)

            def sq_high(G):
                dve.wait_ge(sq_done, G + 1)
                nc.vector.tensor_copy(parts[:, 2, :], x_sq[:]).then_inc(sq_hi_done, 1)

            def sq_low(G):
                dve.wait_ge(sq_hi_done, G + 1)
                nc.vector.tensor_tensor(parts[:, 3, :], x_sq[:], parts[:, 2, :].bitcast(F32),
                                        ALU.subtract).then_inc(sq_lo_done, 1)

            def sum_x(G):
                dve.wait_ge(x_in, 16 * G + 16)
                nc.vector.tensor_reduce(x_sum[:, bass.ds(G * BJ, BJ)], x_cols(G).rearrange("p (j d) -> p j d", d=EMB),
                                        AX_X, ALU.add).then_inc(x_summed, 1)

            def monomials(c, G, g, t, first):
                if t == 0:
                    dve.wait_ge(rep_in[g], 16 * QUADS * (G + 1))
                dve.wait_ge(roll_done, SHIFT_TILES * c + t + 1)
                if not first:
                    if t < SPLIT:
                        dve.wait_ge(lo_ready, SPLIT * (c - 2) + t + 1)
                    else:
                        dve.wait_ge(z_used, SHIFT_TILES * (c - 2) + t + 1)
                b = 2 * (t % 2)
                nc.vector.tensor_tensor(z[:, g % 2, t, :], rolled[:, b:b + 2, :].rearrange("p a b -> p (a b)"),
                                        x_rep[:, g, :], ALU.mult).then_inc(z_done, 1)

            def h_times_q(c, s, G, pair_slot, first):
                dve.wait_ge(q_ready, c + 1)
                if not (first and pair_slot == 0):
                    dve.wait_ge(summed, 2 * G + pair_slot)
                nc.vector.scalar_tensor_tensor(
                    out=hq[UNITS * s:UNITS * (s + 1), pair_slot, :],
                    in0=acc[0:UNITS, 2 * s:2 * s + 2, :].rearrange("p a b -> p (a b)"), scalar=cols[0:UNITS, 0:1],
                    in1=q_sb[0:UNITS, s, :], op0=ALU.add, op1=ALU.mult).then_inc(hq_done, 1)

            def sum_hq(G, pair_slot):
                dve.wait_ge(hq_done, QUADS * G + 2 * pair_slot + 2)
                nc.vector.tensor_reduce(hq_sum[:, pair_slot, bass.ds(G * BJ, BJ)],
                                        hq[:, pair_slot, :].rearrange("p (j d) -> p j d", d=EMB),
                                        AX_X, ALU.add).then_inc(summed, 1)

            nc.vector.memset(low[0:UNITS, 0:2, :], 0.0).then_inc(low_zero, 1)
            dve.wait_ge(cols_in, 32)
            nc.vector.tensor_copy(v_w2[:, FIELDS:FIELDS + 1], cols[0:UNITS, 1:2]).then_inc(v_copied, 1)
            x_low(0)
            sq_high(0)
            sq_low(0)
            dve.wait_ge(rolls_read, 16)
            nc.vector.tensor_copy(rolls[:], rolls_f[:]).then_inc(rolls_ready, 1)
            dve.wait_ge(v_done, 1)
            nc.vector.tensor_copy(v_w2[:, 0:FIELDS], acc[0:UNITS, 0, 0:FIELDS]).then_inc(v_copied, 1)
            nc.vector.tensor_copy(v_rep[:], acc[0:UNITS, 0, 0:FIELDS].unsqueeze(1).to_broadcast((UNITS, QUADS, FIELDS))
                                  ).then_inc(v_copied, 1)
            dve.wait_ge(g_copied, 1)
            g_psum = acc[UNITS:P, :, 0:8 * (FIELDS + 1)].rearrange("p a (b c) -> p a b c", c=FIELDS + 1)
            for k in range(2):
                nc.vector.tensor_copy(low[UNITS:P, k, :].rearrange("p (a b) -> p a b", a=4),
                                      g_psum[:, :, :, FIELDS]).then_inc(low_done, 1)
            dve.wait_ge(w1_in, 16)
            nc.vector.tensor_copy(rows64(wg)[:, :, FIELDS:FIELDS + FIELDS // 2],
                                  rows64(wg)[:, :, 0:FIELDS // 2]).then_inc(wg_doubled, 1)
            nc.vector.tensor_copy(rows64(wgt)[:, :, 0:FIELDS],
                                  rows64(wg)[:, :, 0:FIELDS].rearrange("p r m -> p m r")).then_inc(wg_doubled, 1)
            dve.wait_ge(wg_doubled, 2)
            dve.wait_ge(wgt_done, 1)
            half = FIELDS // 2
            nc.vector.tensor_tensor(sym[:, 0:half - 1, :], diagonals(wg[:])[:, 1:half, :],
                                    diagonals(wgt)[:, 1:half, :], ALU.add).then_inc(sym_done, 1)
            nc.vector.tensor_copy(sym[:, half - 1, :], diagonals(wg[:])[:, half, :]).then_inc(sym_done, 1)
            nc.vector.tensor_copy(low[:, 2:4, :], diagonals(wg[:])[:, 0:1, :].to_broadcast((P, 2, FIELDS))
                                  ).then_inc(low_done, 1)
            for t in range(SHIFT_TILES):
                monomials(0, 0, 0, t, True)
            dve.wait_ge(hi_done, 2)
            nc.vector.tensor_tensor(w_lo[:].rearrange("p t c -> p (t c)"), acc[:, 0, 0:SPLIT * P],
                                    w_hi[:].bitcast(F32).rearrange("p t c -> p (t c)"), ALU.subtract).then_inc(weights_ready, 1)
            nc.vector.tensor_tensor(low_lo[:], acc[:, 1, 0:P], low_hi[:].bitcast(F32), ALU.subtract).then_inc(weights_ready, 1)
            if SPLIT < SHIFT_TILES:
                nc.vector.tensor_copy(w_full[:].rearrange("p t c -> p (t c)"), acc[:, 0, SPLIT * P:]).then_inc(weights_ready, 1)
            dve.wait_ge(cols_late_in, 7 * 16)

            def granule(G, first, last):
                for g in range(QUADS):
                    c = QUADS * G + g
                    nG, ng = (G, g + 1) if g < QUADS - 1 else (G + 1, 0)
                    more = not (last and g == QUADS - 1)
                    if more:
                        monomials(c + 1, nG, ng, 0, first and g == 0)
                        monomials(c + 1, nG, ng, 1, first and g == 0)
                    if not (first and g == 0):
                        h_times_q(c - 1, (g + 1) % 2, G if g else G - 1, ((g + 3) % 4) // 2, first)
                    if g % 2 == 0 and not (first and g == 0):
                        if g == 2:
                            sum_hq(G, 0)
                        else:
                            sum_hq(G - 1, 1)
                    if more:
                        monomials(c + 1, nG, ng, 2, first and g == 0)
                        monomials(c + 1, nG, ng, 3, first and g == 0)
                    if g == 1 and not last:
                        x_low(G + 1)
                        sq_high(G + 1)
                    if g == 2 and not last:
                        sq_low(G + 1)
                    if g == 3:
                        sum_x(G)

            over_granules(dve, granule)
            nc.vector.tensor_copy(b23[:], cols[:, 3:4].to_broadcast((P, P))).then_inc(tail_ready, 1)
            nc.vector.tensor_scalar(w23[:], cols[:, 4:5].to_broadcast((P, QUADS)), float(EMB), None, ALU.mult).then_inc(tail_ready, 1)
            h_times_q(CHUNKS - 1, 1, GRANULES - 1, 1, False)
            sum_hq(GRANULES - 1, 1)
            dve.wait_ge(beta_done, 1)
            nc.vector.tensor_copy(beta[:], rolled[:, 0, 0:1]).then_inc(beta_ready, 1)
            dve.wait_ge(beta_ready, 1)
            nc.vector.tensor_scalar(beta_pick[:], picks[:, 2, :], beta[:, 0:1], None, ALU.mult).then_inc(tail_ready, 1)
            dve.wait_ge(y_done, 1)
            nc.vector.tensor_scalar(y_sb[:], rolled[:, 2, 0:QUADS], cols[:, 5:6], None, ALU.add).then_inc(y_ready, 1)

        @block.tensor
        def _(pe):
            pe.wait_ge(w3_in, 16)
            pe.wait_ge(cols_in, 32)
            w3_v = w3_sb.rearrange("p (h m) -> p m h", m=FIELDS)
            w2_v = w2_sb.rearrange("p (h m) -> p m h", m=FIELDS)
            for m in range(FIELDS):
                mm = nc.tensor.matmul(acc[0:UNITS, 0, m:m + 1], w3_v[:, m, :], cols[0:UNITS, 2:3], start=True, stop=True)
            mm.then_inc(v_done, 1)
            pe.wait_ge(w2_in, 16)
            pe.wait_ge(v_copied, 3)
            for m in range(FIELDS):
                at = (m % 8) * (FIELDS + 1)
                mm = nc.tensor.matmul(acc[UNITS:P, m // 8, at:at + FIELDS + 1], w2_v[:, m, :], v_w2[:], start=True, stop=True)
            mm.then_inc(g_done, 1)

            def roll(c, G, g, t, first):
                if t == 0:
                    pe.wait_ge(stack_in[g], 16 * KINDS * (G + 1))
                if not (first and t < 2):
                    pe.wait_ge(z_done, SHIFT_TILES * c + t - 1)
                for h in range(HALVES):
                    mm = nc.tensor.matmul(rolled[:, 2 * (t % 2) + h, :], rolls[:, t, :],
                                          stack[:, g, h * BANK:(h + 1) * BANK], start=True, stop=True)
                mm.then_inc(roll_done, 1)

            pe.wait_ge(rolls_ready, 1)
            roll(0, 0, 0, 0, True)
            roll(0, 0, 0, 1, True)
            pe.wait_ge(consts_in, 16)
            pe.wait_ge(sym_done, 2)
            for t in range(SHIFT_TILES):
                mm = nc.tensor.transpose(acc[:, 0, t * P:(t + 1) * P],
                                         sym[:, 4 * t:4 * t + 4, :].rearrange("p k m -> p (k m)"), eye[:])
            mm.then_inc(turned, 1)
            pe.wait_ge(low_zero, 1)
            pe.wait_ge(low_done, 3)
            nc.tensor.transpose(acc[:, 1, 0:P], low[:].rearrange("p k m -> p (k m)"), eye[:]).then_inc(turned, 1)
            roll(0, 0, 0, 2, True)
            roll(0, 0, 0, 3, True)
            pe.wait_ge(weights_ready, 2 + (SPLIT < SHIFT_TILES))

            def granule(G, first, last):
                for g in range(QUADS):
                    c, s = QUADS * G + g, g % 2
                    nG, ng = (G, g + 1) if g < QUADS - 1 else (G + 1, 0)

                    def out(h):
                        return acc[:, 2 * s + h, :]

                    if not (first and g < 2):
                        pe.wait_ge(hq_done, c - 1)
                    for h in range(HALVES):
                        cut = stack[:, g, h * BANK:(h + 1) * BANK]
                        nc.tensor.matmul(out(h), low_hi[:], cut, start=True, stop=False)
                        mm = nc.tensor.matmul(out(h), low_lo[:], cut, start=False, stop=False)
                    mm.then_inc(stack_used, 1)
                    for t in range(SHIFT_TILES):
                        if not (last and g == QUADS - 1):
                            roll(c + 1, nG, ng, t, False)
                        end = t == SHIFT_TILES - 1
                        if t < SPLIT:
                            pe.wait_ge(hi_ready, SPLIT * c + t + 1)
                            for h in range(HALVES):
                                cut = z_hi[:, s, t, h * BANK:(h + 1) * BANK]
                                nc.tensor.matmul(out(h), w_hi[:, t, :], cut, start=False, stop=False)
                                nc.tensor.matmul(out(h), w_lo[:, t, :], cut, start=False, stop=False)
                            pe.wait_ge(lo_ready, SPLIT * c + t + 1)
                            for h in range(HALVES):
                                mm = nc.tensor.matmul(out(h), w_hi[:, t, :], z_lo[:, s, t, h * BANK:(h + 1) * BANK],
                                                      start=False, stop=end)
                        else:
                            pe.wait_ge(z_done, SHIFT_TILES * c + t + 1)
                            for h in range(HALVES):
                                mm = nc.tensor.matmul(out(h), w_full[:, t - SPLIT, :], z[:, s, t, h * BANK:(h + 1) * BANK],
                                                      start=False, stop=end)
                        mm.then_inc(z_used, 1)

            over_granules(pe, granule)
            pe.wait_ge(cols_late_in, 7 * 16)
            nc.tensor.matmul(rolled[:, 0, 0:1], v_rep[:].rearrange("p g m -> p (g m)"), cols[0:UNITS, 3:4],
                             start=True, stop=True).then_inc(beta_done, 1)
            pe.wait_ge(summed, 2 * GRANULES)
            pe.wait_ge(x_summed, GRANULES)
            pe.wait_ge(tail_ready, 3)
            out = rolled[:, 2, 0:QUADS]
            nc.tensor.matmul(out, hq_sum[:, 0, :], picks[:, 0, :], start=True, stop=False)
            nc.tensor.matmul(out, hq_sum[:, 1, :], picks[:, 1, :], start=False, stop=False)
            nc.tensor.matmul(out, x_sum[:], beta_pick[:], start=False, stop=False)
            nc.tensor.matmul(out, b23[:], w23[:], start=False, stop=True).then_inc(y_done, 1)


def kernel(r_x0, L0_rec_W1, L0_rec_b1, L0_rec_W2, L0_rec_b2, L0_rec_W3, L0_rec_b3, L0_rec_W_out, L0_rec_b_out):
    import concourse.bacc as bacc
    from concourse.bass_utils import run_bass_kernel_spmd

    names = ["x", "W1", "b1", "W2", "b2", "W3", "b3", "W_out", "b_out"]
    given = [r_x0, L0_rec_W1, L0_rec_b1, L0_rec_W2, L0_rec_b2, L0_rec_W3, L0_rec_b3, L0_rec_W_out, L0_rec_b_out]
    arrays = {n: np.ascontiguousarray(a) for n, a in zip(names, given)}
    arrays["eye_in"], arrays["rolls_in"], arrays["picks_in"] = constants()

    nc = bacc.Bacc("TRN2", target_bir_lowering=False, num_devices=1)
    args = [nc.dram_tensor(n, a.shape, mybir.dt.from_np(a.dtype), kind="ExternalInput").ap() for n, a in arrays.items()]
    y = nc.dram_tensor("y", (arrays["x"].shape[0], 1), F32, kind="ExternalOutput").ap()
    build(nc, *args, y)
    result = run_bass_kernel_spmd(nc, [arrays], core_ids=[0])
    return result.results[0]["y"]
```

```python
from contextlib import ExitStack

import numpy as np

import concourse.bass as bass
from concourse import mybir

F32 = mybir.dt.float32
F32R = mybir.dt.float32r
ALU = mybir.AluOpType
ACT = mybir.ActivationFunctionType
AX_X = mybir.AxisListType.X

P = 128
FIELDS = 32
UNITS = 64
QUADS = P // FIELDS
ROLLS = ((1, 2, 3, 4), (6, 9, 11, 14), (12, 13, 15, 16))
B, C, D = range(3)
AB, AC, BC, AD = range(4)
TILES = 4
SPLIT = 3
BANK = 512


def constants():
    eye = np.eye(P, dtype=np.float32)
    row, col = np.arange(P)[:, None], np.arange(P)[None, :]
    rolls = [
        (row < 2 * FIELDS) & (row % FIELDS == (col % FIELDS + np.array(roll)[col // FIELDS]) % FIELDS)
        for roll in ROLLS
    ]
    g = np.arange(QUADS)[None, :]
    half = row // UNITS
    picks = [(g // 2 == s) & (g % 2 == half) for s in range(2)] + [row // FIELDS == g]
    return eye, np.concatenate(rolls, 1).astype(np.float32), np.concatenate(picks, 1).astype(np.float32)


def build(nc, x, W1, b1, W2, b2, W3, b3, W_out, b_out, eye_in, rolls_in, picks_in, y):
    BATCH, _, EMB = x.shape
    BJ = 16
    COLS = BJ * EMB
    HALVES = COLS // BANK
    GRANULES = BATCH // (QUADS * BJ)
    CHUNKS = GRANULES * QUADS
    MM = FIELDS * FIELDS
    HOM = UNITS * FIELDS
    KINDS = 4

    with ExitStack() as ctx:
        def sb(name, shape, dt=F32):
            return ctx.enter_context(nc.sbuf_tensor(name, shape, dt))

        def sem(name):
            return ctx.enter_context(nc.semaphore(name))

        acc = ctx.enter_context(nc.psum_tensor("acc", [P, 4, BANK], F32))
        rolled = ctx.enter_context(nc.psum_tensor("rolled", [P, 4, BANK], F32))

        x_all = sb("x_all", [P, GRANULES * COLS])
        x_rep = sb("x_rep", [P, QUADS, COLS])
        parts = sb("parts", [P, KINDS, COLS], F32R)
        x_sq = sb("x_sq", [P, COLS])
        stack = sb("stack", [P, QUADS, COLS], F32R)
        z = sb("z", [P, 2, TILES, COLS])
        z_hi = sb("z_hi", [P, 2, SPLIT, COLS], F32R)
        z_lo = sb("z_lo", [P, 2, SPLIT, COLS], F32R)
        b_sb = sb("b_sb", [P, 2, COLS])
        late = sb("late", [P, 4, COLS])
        hq = late[:, 0:2, :]
        q_sb = late[:, 2:4, :]
        hq_sum = sb("hq_sum", [P, 2, GRANULES * BJ])
        x_sum = sb("x_sum", [P, GRANULES * BJ])

        eye = sb("eye", [P, P])
        rolls_f = sb("rolls_f", [P, len(ROLLS), P])
        rolls = sb("rolls", [P, len(ROLLS), P], F32R)
        picks = sb("picks", [P, 3, QUADS])
        cols = sb("cols", [P, 8])
        w3_col = sb("w3_col", [P, 1])
        v_w2 = sb("v_w2", [UNITS, FIELDS + 1])
        v_rep = sb("v_rep", [UNITS, QUADS, FIELDS])
        sym = sb("sym", [P, TILES, QUADS, FIELDS])
        BC0, BC1 = ROLLS[C][0] - ROLLS[B][0], ROLLS[C][3] - ROLLS[B][3]
        sym_bc = sb("sym_bc", [P, BC1 - BC0 + 1, 2 * FIELDS])
        low = sb("low", [P, KINDS, FIELDS])
        w_hi = sb("w_hi", [P, SPLIT, P], F32R)
        w_lo = sb("w_lo", [P, SPLIT, P], F32R)
        w_full = sb("w_full", [P, TILES - SPLIT, P]) if SPLIT < TILES else None
        low_hi = sb("low_hi", [P, P], F32R)
        low_lo = sb("low_lo", [P, P], F32R)
        beta = sb("beta", [P, 1])
        beta_pick = sb("beta_pick", [P, QUADS])
        b23 = sb("b23", [P, P])
        w23 = sb("w23", [P, QUADS])
        y_sb = sb("y_sb", [P, QUADS])

        DIAG = 2 * FIELDS + 1
        setup = z[:, 1, :, :].rearrange("p a b -> p (a b)")
        wg = setup[:, 0:FIELDS * DIAG]
        w2_sb = setup[0:UNITS, 2 * MM:4 * MM]
        w3_sb = setup[UNITS:P, 2 * MM:4 * MM]
        wgt = late[:].rearrange("p a b -> p (a b)")[:, 0:FIELDS * DIAG]

        def rows64(t):
            return t[:, 0:2 * MM].rearrange("p (m c) -> p m c", c=2 * FIELDS)

        def diagonals(t):
            return t.rearrange("p (m c) -> p c m", c=DIAG)

        w3_in, w2_in, w1_in, consts_in = sem("w3_in"), sem("w2_in"), sem("w1_in"), sem("consts_in")
        cols_in, cols_late_in, rolls_read, low_zero = sem("cols_in"), sem("cols_late_in"), sem("rolls_in"), sem("low_zero")
        v_done, v_copied, g_done, g_copied = sem("v_done"), sem("v_copied"), sem("g_done"), sem("g_copied")
        wg_doubled, wgt_done, sym_done, low_done = (
            sem("wg_doubled"), sem("wgt_done"), sem("sym_done"), sem("low_done"))
        table_in, half_done = sem("table_in"), sem("half_done")
        turned, hi_done, weights_ready, rolls_ready = sem("turned"), sem("hi_done"), sem("weights_ready"), sem("rolls_ready")
        x_in = sem("x_in")
        x_hi_done, x_lo_done = sem("x_hi_done"), sem("x_lo_done")
        sq_done, sq_hi_done, sq_lo_done = sem("sq_done"), sem("sq_hi_done"), sem("sq_lo_done")
        stack_in = [sem(f"stack_in{g}") for g in range(QUADS)]
        rep_in = [sem(f"rep_in{g}") for g in range(QUADS)]
        roll_done, b_copied, z_done, hi_ready, lo_ready, z_used = (
            sem("roll_done"), sem("b_copied"), sem("z_done"), sem("hi_ready"), sem("lo_ready"), sem("z_used"))
        stack_used, q_ready, hq_done, summed, x_summed = (
            sem("stack_used"), sem("q_ready"), sem("hq_done"), sem("summed"), sem("x_summed"))
        beta_ready, tail_ready, y_done, y_ready, y_out = (
            sem("beta_ready"), sem("tail_ready"), sem("y_done"), sem("y_ready"), sem("y_out"))

        def over_granules(engine, body):
            body(0, True, False)
            with engine.Fori(1, GRANULES - 1) as G:
                body(G, False, False)
            body(GRANULES - 1, False, True)

        B_SLOT, C_SLOT, D_SLOT = (0, 2), (2, 0), (0, 2)

        G_BANKS, G_FIELDS = 4, FIELDS // 4
        g_psum = acc[UNITS:P, :, 0:G_FIELDS * (FIELDS + 1)].rearrange("p a (b c) -> p a b c", c=FIELDS + 1)

        def x_cols(G):
            return x_all[:, bass.ds(G * COLS, COLS)]

        block = ctx.enter_context(nc.Block())

        @block.sync
        def _(sp):
            x_dram = x.rearrange("(G j g) m d -> G (g m) j d", j=BJ, g=QUADS)

            def load_x(G):
                sp.dma_start(x_cols(G).rearrange("p (j d) -> p j d", d=EMB),
                             x_dram[bass.ds(G, 1)].rearrange("o p j d -> (o p) j d")).then_inc(x_in, 16)

            sp.dma_start(w3_sb, W3.rearrange("o h m -> o (h m)")).then_inc(w3_in, 16)
            load_x(0)
            sp.dma_start(eye[:], eye_in).then_inc(consts_in, 16)
            sp.dma_start(rolls_f[:].rearrange("p t c -> p (t c)"), rolls_in).then_inc(rolls_read, 16)

            def granule(G, first, last):
                sp.wait_ge(x_in, 16 * G + 16)
                for g in range(QUADS):
                    if not first:
                        sp.wait_ge(z_done, TILES * (QUADS * (G - 1) + g + 1))
                    for k in range(QUADS):
                        sp.dma_start(x_rep[FIELDS * k:FIELDS * (k + 1), g, :],
                                     x_all[FIELDS * g:FIELDS * (g + 1), bass.ds(G * COLS, COLS)]).then_inc(rep_in[g], 16)
                    if not first:
                        sp.wait_ge(stack_used, QUADS * (G - 1) + g + 1)
                        sp.nop(nofuse=True)
                    for k, ready in enumerate((x_hi_done, x_lo_done, sq_hi_done, sq_lo_done)):
                        if g == 0:
                            sp.wait_ge(ready, G + 1)
                        sp.dma_start(stack[FIELDS * k:FIELDS * (k + 1), g, :].bitcast(F32),
                                     parts[FIELDS * g:FIELDS * (g + 1), k, :].bitcast(F32)).then_inc(stack_in[g], 16)
                    if g == 0 and not last:
                        load_x(G + 1)

            over_granules(sp, granule)
            sp.wait_ge(y_ready, 1)
            sp.dma_start(y.rearrange("(p g) o -> p (g o)", g=QUADS), y_sb[:]).then_inc(y_out, 16)
            sp.wait_ge(y_out, 16)

        @block.gpsimd
        def _(pool):
            pool.dma_start(picks[:].rearrange("p a b -> p (a b)"), picks_in).then_inc(cols_late_in, 16)
            pool.dma_start(cols[0:UNITS, 3:4], b2.rearrange("(p o) -> p o", o=1)).then_inc(cols_late_in, 16)
            pool.dma_start(cols[UNITS:P, 3:4], b3.rearrange("(p o) -> p o", o=1)).then_inc(cols_late_in, 16)
            pool.dma_start(cols[:, 4:5], W_out[UNITS:3 * UNITS, :]).then_inc(cols_late_in, 16)
            pool.dma_start(cols[:, 5:6], b_out.rearrange("(p o) -> p o", o=1).to_broadcast((P, 1))).then_inc(cols_late_in, 16)
            pool.dma_start(cols[0:UNITS, 0:1], b1.rearrange("(p o) -> p o", o=1)).then_inc(cols_late_in, 16)
            pool.dma_start(cols[UNITS:P, 0:1], W_out[0:UNITS, :]).then_inc(cols_late_in, 16)

            def lows(c, s, first):
                for t in range(SPLIT):
                    pool.wait_ge(hi_ready, SPLIT * c + t + 1)
                    if not first:
                        pool.wait_ge(z_used, TILES * (c - 2) + t + 1)
                    nc.gpsimd.tensor_tensor(z_lo[:, s, t, :], z[:, s, t, :], z_hi[:, s, t, :].bitcast(F32),
                                            ALU.subtract).then_inc(lo_ready, 1)

            def granule(G, first, last):
                for g in range(QUADS):
                    lows(QUADS * G + g, g % 2, first and g < 2)

            over_granules(pool, granule)

        @block.scalar
        def _(act):
            act.dma_start(w3_col[UNITS:P, :], W_out[2 * UNITS:3 * UNITS, :]).then_inc(cols_in, 16)
            act.dma_start(v_w2[:, FIELDS:FIELDS + 1], W_out[UNITS:2 * UNITS, :]).then_inc(cols_in, 16)
            act.dma_start(w2_sb, W2.rearrange("o h m -> o (h m)")).then_inc(w2_in, 16)
            act.dma_start(rows64(wg)[0:UNITS, :, 0:FIELDS], W1).then_inc(w1_in, 16)

            def x_high(G, first):
                act.wait_ge(x_in, 16 * G + 16)
                if not first:
                    for g in range(QUADS):
                        act.wait_ge(stack_in[g], 16 * KINDS * G)
                act.nop(nofuse=True)
                nc.scalar.activation(parts[:, 0, :], x_cols(G), ACT.Copy).then_inc(x_hi_done, 1)

            def square(G, first):
                if not first:
                    act.wait_ge(sq_lo_done, G)
                act.nop(nofuse=True)
                nc.scalar.activation(x_sq[:], x_cols(G), ACT.Square).then_inc(sq_done, 1)

            def highs(c, s, t, first):
                act.wait_ge(z_done, TILES * c + t + 1)
                if not first:
                    act.wait_ge(z_used, TILES * (c - 2) + t + 1)
                nc.scalar.activation(z_hi[:, s, t, :], z[:, s, t, :], ACT.Copy).then_inc(hi_ready, 1)

            def q_out(c, s, first):
                act.wait_ge(z_used, TILES * (c + 1))
                if not first:
                    act.wait_ge(hq_done, c - 1)
                nc.scalar.activation(q_sb[0:UNITS, s, :], acc[UNITS:P, 2 * s:2 * s + 2, :].rearrange("p a b -> p (a b)"),
                                     ACT.Identity, bias=cols[UNITS:P, 0:1]).then_inc(q_ready, 1)

            def copy_b(c, s, first):
                act.wait_ge(roll_done, len(ROLLS) * c + B + 1)
                if not first:
                    act.wait_ge(z_done, TILES * (c - 2) + BC + 1)
                src = B_SLOT[s]
                nc.scalar.activation(b_sb[:, s, :], rolled[:, src:src + 2, :].rearrange("p a b -> p (a b)"),
                                     ACT.Copy).then_inc(b_copied, 1)

            act.wait_ge(low_zero, 1)
            nc.scalar.activation(low[0:UNITS, 2:4, :], low[0:UNITS, 0:2, :], ACT.Square).then_inc(table_in, 1)
            x_high(0, True)
            square(0, True)
            copy_b(0, 0, True)
            for part in range(2):
                act.wait_ge(g_done, part + 1)
                nc.scalar.activation(
                    rows64(wg)[UNITS:P, 16 * part:16 * (part + 1), 0:FIELDS].rearrange("p (a b) c -> p a b c", a=2),
                    g_psum[:, 2 * part:2 * part + 2, :, 0:FIELDS], ACT.Copy).then_inc(g_copied, 1)
                if part == 0:
                    highs(0, 0, AB, True)
            act.wait_ge(g_copied, 2)
            act.wait_ge(w1_in, 16)
            nc.scalar.activation(rows64(wgt)[:, :, FIELDS:FIELDS + FIELDS // 2],
                                 rows64(wg)[:, 0:FIELDS // 2, 0:FIELDS].rearrange("p r m -> p m r"),
                                 ACT.Copy).then_inc(wgt_done, 1)
            highs(0, 0, AC, True)
            highs(0, 0, BC, True)
            act.wait_ge(turned, 2)
            nc.scalar.activation(w_hi[:].rearrange("p t c -> p (t c)"), acc[:, 0, 0:SPLIT * P], ACT.Copy).then_inc(hi_done, 1)
            nc.scalar.activation(low_hi[:], acc[:, 1, 0:P], ACT.Copy).then_inc(hi_done, 1)
            act.wait_ge(cols_late_in, 7 * 16)

            def granule(G, first, last):
                for g in range(QUADS):
                    c = QUADS * G + g
                    if not (last and g == QUADS - 1):
                        copy_b(c + 1, (g + 1) % 2, first and g == 0)
                    if not (first and g == 0):
                        q_out(c - 1, (g + 1) % 2, first and g < 3)
                    if not (last and g == QUADS - 1):
                        highs(c + 1, (g + 1) % 2, AB, first and g == 0)
                        if g == 0 and not last:
                            x_high(G + 1, False)
                        highs(c + 1, (g + 1) % 2, AC, first and g == 0)
                        if g == 0 and not last:
                            square(G + 1, False)
                        highs(c + 1, (g + 1) % 2, BC, first and g == 0)

            over_granules(act, granule)
            for h in range(HALVES):
                act.wait_ge(half_done, h + 1)
                nc.scalar.activation(q_sb[0:UNITS, 1, h * BANK:(h + 1) * BANK], acc[UNITS:P, 2 + h, :],
                                     ACT.Identity, bias=cols[UNITS:P, 0:1]).then_inc(q_ready, 1)

        @block.vector
        def _(dve):
            def x_low(G):
                dve.wait_ge(x_hi_done, G + 1)
                nc.vector.tensor_tensor(parts[:, 1, :], x_cols(G), parts[:, 0, :].bitcast(F32),
                                        ALU.subtract).then_inc(x_lo_done, 1)

            def sq_high(G):
                dve.wait_ge(sq_done, G + 1)
                nc.vector.tensor_copy(parts[:, 2, :], x_sq[:]).then_inc(sq_hi_done, 1)

            def sq_low(G):
                dve.wait_ge(sq_hi_done, G + 1)
                nc.vector.tensor_tensor(parts[:, 3, :], x_sq[:], parts[:, 2, :].bitcast(F32),
                                        ALU.subtract).then_inc(sq_lo_done, 1)

            def sum_x(G):
                dve.wait_ge(x_in, 16 * G + 16)
                nc.vector.tensor_reduce(x_sum[:, bass.ds(G * BJ, BJ)], x_cols(G).rearrange("p (j d) -> p j d", d=EMB),
                                        AX_X, ALU.add).then_inc(x_summed, 1)

            def monomials(c, G, g, t, first):
                if t == 0:
                    dve.wait_ge(rep_in[g], 16 * QUADS * (G + 1))
                if t == AB:
                    dve.wait_ge(b_copied, c + 1)
                if t == AC:
                    dve.wait_ge(roll_done, len(ROLLS) * c + C + 1)
                if t == AD:
                    dve.wait_ge(roll_done, len(ROLLS) * c + D + 1)
                if not first:
                    if t < SPLIT:
                        dve.wait_ge(lo_ready, SPLIT * (c - 2) + t + 1)
                    else:
                        dve.wait_ge(z_used, TILES * (c - 2) + t + 1)
                s = g % 2
                slot = (C_SLOT if t in (AC, BC) else D_SLOT)[s]
                from_psum = rolled[:, slot:slot + 2, :].rearrange("p a b -> p (a b)")
                one = b_sb[:, s, :] if t == AB else from_psum
                other = b_sb[:, s, :] if t == BC else x_rep[:, g, :]
                nc.vector.tensor_tensor(z[:, s, t, :], one, other, ALU.mult).then_inc(z_done, 1)

            def h_times_q(c, s, G, pair_slot, first):
                dve.wait_ge(q_ready, c + 1)
                if not (first and pair_slot == 0):
                    dve.wait_ge(summed, 2 * G + pair_slot)
                nc.vector.scalar_tensor_tensor(
                    out=hq[UNITS * s:UNITS * (s + 1), pair_slot, :],
                    in0=acc[0:UNITS, 2 * s:2 * s + 2, :].rearrange("p a b -> p (a b)"), scalar=cols[0:UNITS, 0:1],
                    in1=q_sb[0:UNITS, s, :], op0=ALU.add, op1=ALU.mult).then_inc(hq_done, 1)

            def sum_hq(G, pair_slot):
                dve.wait_ge(hq_done, QUADS * G + 2 * pair_slot + 2)
                nc.vector.tensor_reduce(hq_sum[:, pair_slot, bass.ds(G * BJ, BJ)],
                                        hq[:, pair_slot, :].rearrange("p (j d) -> p j d", d=EMB),
                                        AX_X, ALU.add).then_inc(summed, 1)

            nc.vector.memset(low[0:UNITS, 0:2, :], 0.0).then_inc(low_zero, 1)
            dve.wait_ge(rolls_read, 16)
            nc.vector.tensor_copy(rolls[:], rolls_f[:]).then_inc(rolls_ready, 1)
            x_low(0)
            sq_high(0)
            sq_low(0)
            dve.wait_ge(v_done, 1)
            nc.vector.tensor_copy(v_w2[:, 0:FIELDS], acc[0:UNITS, 0, 0:FIELDS]).then_inc(v_copied, 1)
            nc.vector.tensor_copy(v_rep[:], acc[0:UNITS, 0, 0:FIELDS].unsqueeze(1).to_broadcast((UNITS, QUADS, FIELDS))
                                  ).then_inc(v_copied, 1)
            monomials(0, 0, 0, AB, True)
            monomials(0, 0, 0, AC, True)
            monomials(0, 0, 0, BC, True)
            dve.wait_ge(g_copied, 2)
            for k in range(2):
                nc.vector.tensor_copy(low[UNITS:P, k, :].rearrange("p (a b) -> p a b", a=G_BANKS),
                                      g_psum[:, :, :, FIELDS]).then_inc(low_done, 1)
            dve.wait_ge(w1_in, 16)
            nc.vector.tensor_copy(rows64(wg)[:, :, FIELDS:FIELDS + FIELDS // 2],
                                  rows64(wg)[:, :, 0:FIELDS // 2]).then_inc(wg_doubled, 1)
            nc.vector.tensor_copy(rows64(wgt)[:, :, 0:FIELDS],
                                  rows64(wg)[:, :, 0:FIELDS].rearrange("p r m -> p m r")).then_inc(wg_doubled, 1)
            dve.wait_ge(wg_doubled, 2)
            dve.wait_ge(wgt_done, 1)
            w_k, wt_k = diagonals(wg), diagonals(wgt)

            def both_orders(to, pick):
                nc.vector.tensor_tensor(to, pick(w_k), pick(wt_k), ALU.add).then_inc(sym_done, 1)

            both_orders(sym[:, AB, :, :], lambda w: w[:, 1:5, :])
            for side in range(2):
                both_orders(sym_bc[:, :, FIELDS * side:FIELDS * (side + 1)], lambda w: w[:, BC0:BC1 + 1, :])
            both_orders(sym[:, AC, :, :].rearrange("p (a k) m -> p a k m", a=2),
                        lambda w: w[:, 6:16, :].rearrange("p (a k) m -> p a k m", a=2)[:, :, 0:4:3, :])
            both_orders(sym[:, AD, 0:2, :], lambda w: w[:, 12:14, :])
            both_orders(sym[:, AD, 2:3, :], lambda w: w[:, 15:16, :])
            nc.vector.tensor_copy(sym[:, AD, 3:4, :], w_k[:, 16:17, :]).then_inc(sym_done, 1)
            dve.wait_ge(table_in, 1)
            nc.vector.tensor_copy(low[:, 2:4, :], w_k[:, 0:1, :].to_broadcast((P, 2, FIELDS))).then_inc(low_done, 1)
            dve.wait_ge(sym_done, 3)
            for j in range(QUADS):
                b = ROLLS[B][j]
                nc.vector.tensor_copy(sym[:, BC, j, :], sym_bc[:, ROLLS[C][j] - b - BC0, b:b + FIELDS]).then_inc(sym_done, 1)
            monomials(0, 0, 0, AD, True)
            dve.wait_ge(hi_done, 2)
            nc.vector.tensor_tensor(w_lo[:].rearrange("p t c -> p (t c)"), acc[:, 0, 0:SPLIT * P],
                                    w_hi[:].bitcast(F32).rearrange("p t c -> p (t c)"), ALU.subtract).then_inc(weights_ready, 1)
            nc.vector.tensor_tensor(low_lo[:], acc[:, 1, 0:P], low_hi[:].bitcast(F32), ALU.subtract).then_inc(weights_ready, 1)
            if SPLIT < TILES:
                nc.vector.tensor_copy(w_full[:].rearrange("p t c -> p (t c)"), acc[:, 0, SPLIT * P:]).then_inc(weights_ready, 1)
            nc.vector.tensor_copy(beta[:], acc[:, 1, 2 * P:2 * P + 1]).then_inc(beta_ready, 1)
            dve.wait_ge(beta_ready, 1)
            dve.wait_ge(cols_late_in, 7 * 16)
            nc.vector.tensor_scalar(beta_pick[:], picks[:, 2, :], beta[:, 0:1], None, ALU.mult).then_inc(tail_ready, 1)
            nc.vector.tensor_copy(b23[:], cols[:, 3:4].to_broadcast((P, P))).then_inc(tail_ready, 1)
            nc.vector.tensor_scalar(w23[:], cols[:, 4:5].to_broadcast((P, QUADS)), float(EMB), None, ALU.mult).then_inc(tail_ready, 1)

            def granule(G, first, last):
                for g in range(QUADS):
                    c = QUADS * G + g
                    nG, ng = (G, g + 1) if g < QUADS - 1 else (G + 1, 0)
                    more = not (last and g == QUADS - 1)
                    if more:
                        monomials(c + 1, nG, ng, AB, first and g == 0)
                        monomials(c + 1, nG, ng, AC, first and g == 0)
                    if g == 1 and not last:
                        sq_high(G + 1)
                    if not (first and g == 0):
                        h_times_q(c - 1, (g + 1) % 2, G if g else G - 1, ((g + 3) % 4) // 2, first)
                    if more:
                        monomials(c + 1, nG, ng, BC, first and g == 0)
                        monomials(c + 1, nG, ng, AD, first and g == 0)
                    if g % 2 == 0 and not (first and g == 0):
                        if g == 2:
                            sum_hq(G, 0)
                        else:
                            sum_hq(G - 1, 1)
                    if g == 0 and not last:
                        x_low(G + 1)
                    if g == 1 and not last:
                        sq_low(G + 1)
                    if g == 3:
                        sum_x(G)

            over_granules(dve, granule)
            for h in range(HALVES):
                cut = slice(h * BANK, (h + 1) * BANK)
                dve.wait_ge(q_ready, CHUNKS + h)
                if h == 0:
                    dve.wait_ge(summed, 2 * GRANULES - 1)
                nc.vector.scalar_tensor_tensor(
                    out=hq[UNITS:P, 1, cut], in0=acc[0:UNITS, 2 + h, :], scalar=cols[0:UNITS, 0:1],
                    in1=q_sb[0:UNITS, 1, cut], op0=ALU.add, op1=ALU.mult).then_inc(hq_done, 1)
                dve.wait_ge(hq_done, CHUNKS + h)
                at = (GRANULES - 1) * BJ + h * BJ // HALVES
                nc.vector.tensor_reduce(hq_sum[:, 1, at:at + BJ // HALVES], hq[:, 1, cut].rearrange("p (j d) -> p j d", d=EMB),
                                        AX_X, ALU.add).then_inc(summed, 1)
            dve.wait_ge(y_done, 1)
            nc.vector.tensor_scalar(y_sb[:], rolled[:, 2, 0:QUADS], cols[:, 5:6], None, ALU.add).then_inc(y_ready, 1)

        @block.tensor
        def _(pe):
            pe.wait_ge(w3_in, 16)
            pe.wait_ge(cols_in, 32)
            w3_v = w3_sb.rearrange("p (h m) -> p m h", m=FIELDS)
            w2_v = w2_sb.rearrange("p (h m) -> p m h", m=FIELDS)
            for m in range(FIELDS):
                mm = nc.tensor.matmul(acc[0:UNITS, 0, m:m + 1], w3_v[:, m, :], w3_col[UNITS:P, :], start=True, stop=True)
            mm.then_inc(v_done, 1)

            def g_and_l(fields):
                for m in fields:
                    at = (m % G_FIELDS) * (FIELDS + 1)
                    mm = nc.tensor.matmul(acc[UNITS:P, m // G_FIELDS, at:at + FIELDS + 1], w2_v[:, m, :], v_w2[:],
                                          start=True, stop=True)
                return mm

            def roll(c, G, g, i, first):
                if i == B:
                    pe.wait_ge(stack_in[g], 16 * KINDS * (G + 1))
                    if not first:
                        pe.wait_ge(z_done, TILES * (c - 1) + BC + 1)
                if i == C and not first:
                    pe.wait_ge(z_done, TILES * (c - 1) + AD + 1)
                if i == D:
                    pe.wait_ge(b_copied, c + 1)
                slot = (B_SLOT, C_SLOT, D_SLOT)[i][g % 2]
                for h in range(HALVES):
                    mm = nc.tensor.matmul(rolled[:, slot + h, :], rolls[:, i, :],
                                          stack[:, g, h * BANK:(h + 1) * BANK], start=True, stop=True)
                mm.then_inc(roll_done, 1)

            pe.wait_ge(w2_in, 16)
            pe.wait_ge(v_copied, 2)
            g_and_l(range(0, 8))
            pe.wait_ge(rolls_ready, 1)
            roll(0, 0, 0, B, True)
            g_and_l(range(8, 16)).then_inc(g_done, 1)
            roll(0, 0, 0, C, True)
            g_and_l(range(16, 32)).then_inc(g_done, 1)
            roll(0, 0, 0, D, True)
            pe.wait_ge(consts_in, 16)
            pe.wait_ge(low_zero, 1)
            pe.wait_ge(low_done, 3)
            nc.tensor.transpose(acc[:, 1, 0:P], low[:].rearrange("p k m -> p (k m)"), eye[:]).then_inc(turned, 1)
            pe.wait_ge(cols_late_in, 7 * 16)
            nc.tensor.matmul(acc[:, 1, 2 * P:2 * P + 1], v_rep[:].rearrange("p g m -> p (g m)"), cols[0:UNITS, 3:4],
                             start=True, stop=True)
            pe.wait_ge(sym_done, 7 + QUADS)
            for t in range(TILES):
                mm = nc.tensor.transpose(acc[:, 0, t * P:(t + 1) * P], sym[:, t, :, :].rearrange("p k m -> p (k m)"), eye[:])
            mm.then_inc(turned, 1)
            pe.wait_ge(weights_ready, 2 + (SPLIT < TILES))
            pe.wait_ge(beta_ready, 1)

            def by_halves(c, g, s, out):
                pe.wait_ge(hq_done, c - 1)
                for h in range(HALVES):
                    cut = slice(h * BANK, (h + 1) * BANK)
                    nc.tensor.matmul(out(h), low_hi[:], stack[:, g, cut], start=True, stop=False)
                    nc.tensor.matmul(out(h), low_lo[:], stack[:, g, cut], start=False, stop=False)
                    for t in range(SPLIT):
                        if h == 0:
                            pe.wait_ge(hi_ready, SPLIT * c + t + 1)
                        nc.tensor.matmul(out(h), w_hi[:, t, :], z_hi[:, s, t, cut], start=False, stop=False)
                        nc.tensor.matmul(out(h), w_lo[:, t, :], z_hi[:, s, t, cut], start=False, stop=False)
                        if h == 0:
                            pe.wait_ge(lo_ready, SPLIT * c + t + 1)
                        mm = nc.tensor.matmul(out(h), w_hi[:, t, :], z_lo[:, s, t, cut], start=False, stop=t == TILES - 1)
                    for t in range(SPLIT, TILES):
                        if h == 0:
                            pe.wait_ge(z_done, TILES * c + t + 1)
                        mm = nc.tensor.matmul(out(h), w_full[:, t - SPLIT, :], z[:, s, t, cut], start=False, stop=t == TILES - 1)
                    mm.then_inc(half_done, 1)

            def granule(G, first, last):
                for g in range(QUADS):
                    c, s = QUADS * G + g, g % 2
                    nG, ng = (G, g + 1) if g < QUADS - 1 else (G + 1, 0)

                    def out(h):
                        return acc[:, 2 * s + h, :]

                    if last and g == QUADS - 1:
                        by_halves(c, g, s, out)
                        continue
                    roll(c + 1, nG, ng, B, False)
                    if not (first and g < 2):
                        pe.wait_ge(hq_done, c - 1)
                    for h in range(HALVES):
                        cut = stack[:, g, h * BANK:(h + 1) * BANK]
                        nc.tensor.matmul(out(h), low_hi[:], cut, start=True, stop=False)
                        mm = nc.tensor.matmul(out(h), low_lo[:], cut, start=False, stop=False)
                    mm.then_inc(stack_used, 1)
                    roll(c + 1, nG, ng, C, False)
                    for t in range(TILES):
                        if t == AC:
                            roll(c + 1, nG, ng, D, False)
                        end = t == TILES - 1
                        if t < SPLIT:
                            pe.wait_ge(hi_ready, SPLIT * c + t + 1)
                            for h in range(HALVES):
                                cut = z_hi[:, s, t, h * BANK:(h + 1) * BANK]
                                nc.tensor.matmul(out(h), w_hi[:, t, :], cut, start=False, stop=False)
                                nc.tensor.matmul(out(h), w_lo[:, t, :], cut, start=False, stop=False)
                            pe.wait_ge(lo_ready, SPLIT * c + t + 1)
                            for h in range(HALVES):
                                mm = nc.tensor.matmul(out(h), w_hi[:, t, :], z_lo[:, s, t, h * BANK:(h + 1) * BANK],
                                                      start=False, stop=end)
                        else:
                            pe.wait_ge(z_done, TILES * c + t + 1)
                            for h in range(HALVES):
                                mm = nc.tensor.matmul(out(h), w_full[:, t - SPLIT, :], z[:, s, t, h * BANK:(h + 1) * BANK],
                                                      start=False, stop=end)
                        mm.then_inc(z_used, 1)

            over_granules(pe, granule)
            pe.wait_ge(tail_ready, 3)
            pe.wait_ge(x_summed, GRANULES)
            out = rolled[:, 2, 0:QUADS]
            nc.tensor.matmul(out, b23[:], w23[:], start=True, stop=False)
            nc.tensor.matmul(out, x_sum[:], beta_pick[:], start=False, stop=False)
            pe.wait_ge(summed, 2 * GRANULES - 1)
            nc.tensor.matmul(out, hq_sum[:, 0, :], picks[:, 0, :], start=False, stop=False)
            pe.wait_ge(summed, 2 * GRANULES + 1)
            nc.tensor.matmul(out, hq_sum[:, 1, :], picks[:, 1, :], start=False, stop=True).then_inc(y_done, 1)


def kernel(r_x0, L0_rec_W1, L0_rec_b1, L0_rec_W2, L0_rec_b2, L0_rec_W3, L0_rec_b3, L0_rec_W_out, L0_rec_b_out):
    import concourse.bacc as bacc
    from concourse.bass_utils import run_bass_kernel_spmd

    names = ["x", "W1", "b1", "W2", "b2", "W3", "b3", "W_out", "b_out"]
    given = [r_x0, L0_rec_W1, L0_rec_b1, L0_rec_W2, L0_rec_b2, L0_rec_W3, L0_rec_b3, L0_rec_W_out, L0_rec_b_out]
    arrays = {n: np.ascontiguousarray(a) for n, a in zip(names, given)}
    arrays["eye_in"], arrays["rolls_in"], arrays["picks_in"] = constants()

    nc = bacc.Bacc("TRN2", target_bir_lowering=False, num_devices=1)
    args = [nc.dram_tensor(n, a.shape, mybir.dt.from_np(a.dtype), kind="ExternalInput").ap() for n, a in arrays.items()]
    y = nc.dram_tensor("y", (arrays["x"].shape[0], 1), F32, kind="ExternalOutput").ap()
    build(nc, *args, y)
    result = run_bass_kernel_spmd(nc, [arrays], core_ids=[0])
    return result.results[0]["y"]
```

```python
from contextlib import ExitStack

import numpy as np

import concourse.bass as bass
from concourse import mybir

F32 = mybir.dt.float32
F32R = mybir.dt.float32r
ALU = mybir.AluOpType
ACT = mybir.ActivationFunctionType
AX_X = mybir.AxisListType.X

P = 128
FIELDS = 32
UNITS = 64
QUADS = P // FIELDS
ROLLS = ((1, 2, 3, 4), (6, 9, 11, 14), (12, 13, 15, 16))
B, C, D = range(3)
AB, AC, DD, BC = range(4)
TILES = 4
PRODUCTS = (AB, AC, BC)
TURN = {t: n + 1 for n, t in enumerate(PRODUCTS)}
HI_TURN = {DD: 1, AB: 2, AC: 3, BC: 4}
BANK = 512


def constants():
    row, col = np.arange(P)[:, None], np.arange(P)[None, :]
    own = row % FIELDS == col % FIELDS
    rolled_c, rolled_d = (row % FIELDS == (col % FIELDS + np.array(ROLLS[i])[col // FIELDS]) % FIELDS for i in (C, D))
    is_x = row < 2 * FIELDS
    rolls = np.concatenate([is_x & rolled_c, is_x & (own | rolled_d)], 1)
    excess = -1.0 * (col >= 2 * FIELDS) * (own | rolled_d.T)
    turns = np.concatenate([np.eye(P), np.eye(P) / 2, excess], 1)
    g = np.arange(QUADS)[None, :]
    half = row // UNITS
    picks = [(g // 2 == s) & (g % 2 == half) for s in range(2)] + [row // FIELDS == g]
    return turns.astype(np.float32), rolls.astype(np.float32), np.concatenate(picks, 1).astype(np.float32)


def build(nc, x, W1, b1, W2, b2, W3, b3, W_out, b_out, turns_in, rolls_in, picks_in, y):
    BATCH, _, EMB = x.shape
    BJ = 16
    COLS = BJ * EMB
    HALVES = COLS // BANK
    GRANULES = BATCH // (QUADS * BJ)
    CHUNKS = GRANULES * QUADS
    MM = FIELDS * FIELDS
    HOM = UNITS * FIELDS
    PAIRS = QUADS // 2
    KINDS = 4

    with ExitStack() as ctx:
        def sb(name, shape, dt=F32):
            return ctx.enter_context(nc.sbuf_tensor(name, shape, dt))

        def sem(name):
            return ctx.enter_context(nc.semaphore(name))

        acc = ctx.enter_context(nc.psum_tensor("acc", [P, 4, BANK], F32))
        rolled = ctx.enter_context(nc.psum_tensor("rolled", [P, 2, HALVES, BANK], F32))

        x_all = sb("x_all", [P, GRANULES * COLS])
        x_rep = sb("x_rep", [P, QUADS, COLS])
        b_rep = sb("b_rep", [P, QUADS, COLS])
        parts = sb("parts", [P, KINDS, COLS])
        stack = sb("stack", [P, QUADS, COLS], F32R)
        z = sb("z", [P, TILES, COLS])
        z_hi = sb("z_hi", [P, 2, TILES, COLS], F32R)
        z_lo = sb("z_lo", [P, 2, TILES, COLS], F32R)
        late = sb("late", [P, 4, COLS])
        hq = late[:, 0:2, :]
        q_sb = late[:, 2:4, :]
        hq_sum = sb("hq_sum", [P, 2, GRANULES * BJ])
        x_sum = sb("x_sum", [P, GRANULES * BJ])

        turns = sb("turns", [P, 3, P])
        eye, eye_half, excess = (turns[:, i, :] for i in range(3))
        rolls = sb("rolls", [P, 2, P], F32R)
        picks = sb("picks", [P, 3, QUADS])
        cols = sb("cols", [P, 8])
        w3_col = sb("w3_col", [P, 1])
        v_w2 = sb("v_w2", [UNITS, FIELDS + 1])
        v_rep = sb("v_rep", [UNITS, QUADS, FIELDS])
        low = sb("low", [P, KINDS, FIELDS])
        w_hi = sb("w_hi", [P, TILES, P], F32R)
        w_lo = sb("w_lo", [P, TILES, P], F32R)
        w_dd = sb("w_dd", [P, P])
        low_hi = sb("low_hi", [P, P], F32R)
        low_lo = sb("low_lo", [P, P], F32R)
        beta = sb("beta", [P, 1])
        beta_pick = sb("beta_pick", [P, QUADS])
        b23 = sb("b23", [P, P])
        w23 = sb("w23", [P, QUADS])
        y_sb = sb("y_sb", [P, QUADS])

        DIAG = 2 * FIELDS + 1
        setup = x_all[:, 3 * COLS:]
        wg = setup[:, 0:FIELDS * DIAG]
        w2_sb = setup[0:UNITS, 2 * MM:4 * MM]
        w3_sb = setup[UNITS:P, 2 * MM:4 * MM]
        sym = setup[:, 4 * MM:4 * MM + TILES * P].rearrange("p (t k m) -> p t k m", k=QUADS, m=FIELDS)
        BC0, BC1 = ROLLS[C][0] - ROLLS[B][0], ROLLS[C][3] - ROLLS[B][3]
        sym_bc = setup[:, 4 * MM + TILES * P:4 * MM + TILES * P + (BC1 - BC0 + 1) * 2 * FIELDS].rearrange(
            "p (k m) -> p k m", m=2 * FIELDS)
        rolls_f = parts[:, 3, 0:2 * P]
        wgt = late[:].rearrange("p a b -> p (a b)")[:, 0:FIELDS * DIAG]

        def rows64(t):
            return t[:, 0:2 * MM].rearrange("p (m c) -> p m c", c=2 * FIELDS)

        def diagonals(t):
            return t.rearrange("p (m c) -> p c m", c=DIAG)

        w3_in, w2_in, w1_in, consts_in = sem("w3_in"), sem("w2_in"), sem("w1_in"), sem("consts_in")
        w3_col_in, w2_col_in, cols_late_in = sem("w3_col_in"), sem("w2_col_in"), sem("cols_late_in")
        rolls_read, low_zero = sem("rolls_read"), sem("low_zero")
        v_done, v_copied, g_done, g_copied = sem("v_done"), sem("v_copied"), sem("g_done"), sem("g_copied")
        wg_doubled, wgt_done, sym_done, low_done = (
            sem("wg_doubled"), sem("wgt_done"), sem("sym_done"), sem("low_done"))
        table_in, half_done, final_lo_ready = sem("table_in"), sem("half_done"), sem("final_lo_ready")
        dd_turned, dd_copied, turned, low_turned = sem("dd_turned"), sem("dd_copied"), sem("turned"), sem("low_turned")
        hi_done, weights_ready, rolls_ready = sem("hi_done"), sem("weights_ready"), sem("rolls_ready")
        x_in = sem("x_in")
        x_hi_done, x_lo_done = sem("x_hi_done"), sem("x_lo_done")
        sq_done, sq_hi_done, sq_lo_done = sem("sq_done"), sem("sq_hi_done"), sem("sq_lo_done")
        stack_in = [sem(f"stack_in{g}") for g in range(QUADS)]
        first_in = [sem(f"first_in{p}") for p in range(PAIRS)]
        rep_in = [sem(f"rep_in{p}") for p in range(PAIRS)]
        b_in = [sem(f"b_in{p}") for p in range(PAIRS)]
        early_first_in, early_rep_in, early_b_in, early_b_rest_in, second_rep_in = (
            sem("early_first_in"), sem("early_rep_in"), sem("early_b_in"), sem("early_b_rest_in"), sem("second_rep_in"))

        def pairs_in(G, p):
            return G + 1 - (p == 0)

        c_rolled, d_rolled, squared, z_done = sem("c_rolled"), sem("d_rolled"), sem("squared"), sem("z_done")
        hi_ready, lo_ready, square_lo_ready, z_used = (
            sem("hi_ready"), sem("lo_ready"), sem("square_lo_ready"), sem("z_used"))
        stack_used, q_ready, hq_done, summed, x_summed = (
            sem("stack_used"), sem("q_ready"), sem("hq_done"), sem("summed"), sem("x_summed"))
        beta_ready, tail_ready, y_done, y_ready, y_out = (
            sem("beta_ready"), sem("tail_ready"), sem("y_done"), sem("y_ready"), sem("y_out"))

        def over_granules(engine, body):
            body(0, True, False)
            with engine.Fori(1, GRANULES - 1) as G:
                body(G, False, False)
            body(GRANULES - 1, False, True)

        G_BANKS, G_FIELDS = 4, FIELDS // 4
        g_psum = acc[UNITS:P, :, 0:G_FIELDS * (FIELDS + 1)].rearrange("p a (b c) -> p a b c", c=FIELDS + 1)

        def x_cols(G):
            return x_all[:, bass.ds(G * COLS, COLS)]

        block = ctx.enter_context(nc.Block())

        @block.sync
        def _(sp):
            x_dram = x.rearrange("(G j g) m d -> G (g m) j d", j=BJ, g=QUADS)

            def load_x(G):
                sp.dma_start(x_cols(G).rearrange("p (j d) -> p j d", d=EMB),
                             x_dram[bass.ds(G, 1)].rearrange("o p j d -> (o p) j d")).then_inc(x_in, 16)

            sp.dma_start(w3_sb, W3.rearrange("o h m -> o (h m)")).then_inc(w3_in, 16)
            load_x(0)
            sp.dma_start(rolls_f, rolls_in).then_inc(rolls_read, 16)

            def first_quadrant(G, p, first):
                if not first:
                    sp.wait_ge(z_done, len(PRODUCTS) * (QUADS * (G - 1) + 2 * p + 1) + TURN[AC])
                    sp.nop(nofuse=True)
                for g in (2 * p, 2 * p + 1):
                    sp.dma_start(x_rep[0:FIELDS, g, :],
                                 x_all[FIELDS * g:FIELDS * (g + 1), bass.ds(G * COLS, COLS)]).then_inc(first_in[p], 16)

            def other_quadrants(G, p):
                sp.wait_ge(first_in[p], 32 * pairs_in(G, p))
                sp.nop(nofuse=True)
                pair = slice(2 * p, 2 * p + 2)
                for k in range(1, QUADS):
                    sp.dma_start(x_rep[FIELDS * k:FIELDS * (k + 1), pair, :], x_rep[0:FIELDS, pair, :]).then_inc(rep_in[p], 16)

            def b_tiles(G, p, first):
                if not first:
                    sp.wait_ge(z_done, len(PRODUCTS) * (QUADS * (G - 1) + 2 * p + 2))
                    sp.nop(nofuse=True)
                sp.wait_ge(rep_in[p], 16 * (QUADS - 1) * pairs_in(G, p))
                sp.nop(nofuse=True)
                pair = slice(2 * p, 2 * p + 2)
                for k, roll in enumerate(ROLLS[B]):
                    sp.dma_start(b_rep[FIELDS * k:FIELDS * (k + 1), pair, :],
                                 x_rep[roll:roll + FIELDS, pair, :]).then_inc(b_in[p], 16)

            def stack_kinds(G, g, first, kinds=range(KINDS)):
                if not first:
                    sp.wait_ge(stack_used, QUADS * (G - 1) + g + 1)
                    sp.nop(nofuse=True)
                for k in kinds:
                    if g == 0:
                        sp.wait_ge((x_hi_done, x_lo_done, sq_hi_done, sq_lo_done)[k], G + 1)
                        sp.nop(nofuse=True)
                    sp.dma_start(stack[FIELDS * k:FIELDS * (k + 1), g, :].bitcast(F32),
                                 parts[FIELDS * g:FIELDS * (g + 1), k, :]).then_inc(stack_in[g], 16)

            def first_pair():
                sp.wait_ge(x_in, 16)
                for k in range(2):
                    sp.dma_start(x_rep[FIELDS * k:FIELDS * (k + 1), 0, :], x_all[0:FIELDS, 0:COLS]).then_inc(early_first_in, 16)
                stack_kinds(0, 0, True, range(3))
                sp.wait_ge(early_first_in, 32)
                for k in range(2):
                    roll = ROLLS[B][k]
                    sp.dma_start(b_rep[FIELDS * k:FIELDS * (k + 1), 0, :], x_rep[roll:roll + FIELDS, 0, :]).then_inc(early_b_in, 16)
                stack_kinds(0, 0, True, range(3, KINDS))
                sp.dma_start(rows64(wg)[0:UNITS, :, 0:FIELDS], W1).then_inc(w1_in, 16)
                sp.dma_start(turns[:].rearrange("p t c -> p (t c)"), turns_in).then_inc(consts_in, 16)
                stack_kinds(0, 1, True)
                load_x(1)
                sp.wait_ge(second_rep_in, 16 * QUADS)
                for k, roll in enumerate(ROLLS[B]):
                    sp.dma_start(b_rep[FIELDS * k:FIELDS * (k + 1), 1, :], x_rep[roll:roll + FIELDS, 1, :]).then_inc(b_in[0], 16)

            def granule(G, first, last):
                if first:
                    first_pair()
                else:
                    other_quadrants(G, 0)
                    b_tiles(G, 0, first)
                    stack_kinds(G, 0, first)
                    if not last:
                        load_x(G + 1)
                    stack_kinds(G, 1, first)
                first_quadrant(G, 1, first)
                stack_kinds(G, 2, first)
                other_quadrants(G, 1)
                stack_kinds(G, 3, first)
                b_tiles(G, 1, first)
                if not last:
                    sp.wait_ge(x_in, 16 * (G + 2))
                    sp.nop(nofuse=True)
                    first_quadrant(G + 1, 0, False)

            over_granules(sp, granule)
            sp.wait_ge(y_ready, 1)
            sp.dma_start(y.rearrange("(p g) o -> p (g o)", g=QUADS), y_sb[:]).then_inc(y_out, 16)
            sp.wait_ge(y_out, 16)

        @block.gpsimd
        def _(pool):
            pool.dma_start(picks[:].rearrange("p a b -> p (a b)"), picks_in).then_inc(cols_late_in, 16)
            pool.dma_start(cols[0:UNITS, 3:4], b2.rearrange("(p o) -> p o", o=1)).then_inc(cols_late_in, 16)
            pool.dma_start(cols[UNITS:P, 3:4], b3.rearrange("(p o) -> p o", o=1)).then_inc(cols_late_in, 16)
            pool.dma_start(cols[:, 4:5], W_out[UNITS:3 * UNITS, :]).then_inc(cols_late_in, 16)
            pool.dma_start(cols[:, 5:6], b_out.rearrange("(p o) -> p o", o=1).to_broadcast((P, 1))).then_inc(cols_late_in, 16)
            pool.dma_start(cols[0:UNITS, 0:1], b1.rearrange("(p o) -> p o", o=1)).then_inc(cols_late_in, 16)
            pool.dma_start(cols[UNITS:P, 0:1], W_out[0:UNITS, :]).then_inc(cols_late_in, 16)

            pool.wait_ge(x_in, 16)
            for k in range(2, QUADS):
                pool.dma_start(x_rep[FIELDS * k:FIELDS * (k + 1), 0, :], x_all[0:FIELDS, 0:COLS]).then_inc(early_rep_in, 16)
            pool.wait_ge(early_first_in, 32)
            for k in range(2, QUADS):
                roll = ROLLS[B][k]
                pool.dma_start(b_rep[FIELDS * k:FIELDS * (k + 1), 0, :], x_rep[roll:roll + FIELDS, 0, :]
                               ).then_inc(early_b_rest_in, 16)
            for k in range(QUADS):
                pool.dma_start(x_rep[FIELDS * k:FIELDS * (k + 1), 1, :], x_all[FIELDS:2 * FIELDS, 0:COLS]).then_inc(second_rep_in, 16)

            def lows(c, s, first, final):
                for t in (AB, BC) if final else PRODUCTS:
                    pool.wait_ge(hi_ready, TILES * c + HI_TURN[t])
                    if not first:
                        pool.wait_ge(z_used, TILES * (c - 2) + t + 1)
                    nc.gpsimd.tensor_tensor(z_lo[:, s, t, :], z[:, t, :], z_hi[:, s, t, :].bitcast(F32),
                                            ALU.subtract).then_inc(lo_ready, 1)

            def granule(G, first, last):
                for g in range(QUADS):
                    lows(QUADS * G + g, g % 2, first and g < 2, last and g == QUADS - 1)

            over_granules(pool, granule)

        @block.scalar
        def _(act):
            act.dma_start(w3_col[UNITS:P, :], W_out[2 * UNITS:3 * UNITS, :]).then_inc(w3_col_in, 16)
            act.dma_start(v_w2[:, FIELDS:FIELDS + 1], W_out[UNITS:2 * UNITS, :]).then_inc(w2_col_in, 16)
            act.dma_start(w2_sb, W2.rearrange("o h m -> o (h m)")).then_inc(w2_in, 16)

            def x_high(G, first):
                act.wait_ge(x_in, 16 * G + 16)
                if not first:
                    for g in range(QUADS):
                        act.wait_ge(stack_in[g], 16 * KINDS * G)
                act.nop(nofuse=True)
                nc.scalar.activation(parts[:, 0, :].bitcast(F32R), x_cols(G), ACT.Copy).then_inc(x_hi_done, 1)

            def square_high(G):
                nc.scalar.activation(parts[:, 2, :].bitcast(F32R), x_cols(G), ACT.Square).then_inc(sq_hi_done, 1)

            def square_full(G):
                nc.scalar.activation(parts[:, 3, :], x_cols(G), ACT.Square).then_inc(sq_done, 1)

            def highs(c, s, t, first):
                act.wait_ge(z_done, len(PRODUCTS) * c + TURN[t])
                if not first:
                    act.wait_ge(z_used, TILES * (c - 2) + t + 1)
                nc.scalar.activation(z_hi[:, s, t, :], z[:, t, :], ACT.Copy).then_inc(hi_ready, 1)

            def dd_rounded(c, s, first):
                act.wait_ge(d_rolled, c + 1)
                if not first:
                    act.wait_ge(z_used, TILES * (c - 2) + DD + 1)
                nc.scalar.activation(z_hi[:, s, DD, :], rolled[:, 1, :, :].rearrange("p a b -> p (a b)"),
                                     ACT.Square).then_inc(hi_ready, 1)

            def dd_full(c, first):
                if not first:
                    act.wait_ge(square_lo_ready, c)
                nc.scalar.activation(z[:, DD, :], rolled[:, 1, :, :].rearrange("p a b -> p (a b)"),
                                     ACT.Square).then_inc(squared, 1)

            def q_out(c, s, first):
                act.wait_ge(z_used, TILES * (c + 1))
                if not first:
                    act.wait_ge(hq_done, c - 1)
                nc.scalar.activation(q_sb[0:UNITS, s, :], acc[UNITS:P, 2 * s:2 * s + 2, :].rearrange("p a b -> p (a b)"),
                                     ACT.Identity, bias=cols[UNITS:P, 0:1]).then_inc(q_ready, 1)

            act.wait_ge(low_zero, 1)
            nc.scalar.activation(low[0:UNITS, 2:4, :], low[0:UNITS, 0:2, :], ACT.Square).then_inc(table_in, 1)
            x_high(0, True)
            act.wait_ge(rolls_ready, 1)
            square_high(0)
            square_full(0)

            def g_out(part):
                act.wait_ge(g_done, part + 1)
                nc.scalar.activation(
                    rows64(wg)[UNITS:P, 16 * part:16 * (part + 1), 0:FIELDS].rearrange("p (a b) c -> p a b c", a=2),
                    g_psum[:, 2 * part:2 * part + 2, :, 0:FIELDS], ACT.Copy).then_inc(g_copied, 1)

            g_out(0)
            dd_rounded(0, 0, True)
            highs(0, 0, AB, True)
            g_out(1)
            act.wait_ge(g_copied, 2)
            act.wait_ge(w1_in, 16)
            nc.scalar.activation(rows64(wgt)[:, :, FIELDS:FIELDS + FIELDS // 2],
                                 rows64(wg)[:, 0:FIELDS // 2, 0:FIELDS].rearrange("p r m -> p m r"),
                                 ACT.Copy).then_inc(wgt_done, 1)
            dd_full(0, True)
            highs(0, 0, AC, True)
            act.wait_ge(low_turned, 1)
            nc.scalar.activation(low_hi[:], acc[:, 3, 0:P], ACT.Copy).then_inc(hi_done, 1)
            act.wait_ge(turned, 1)
            nc.scalar.activation(w_hi[:].rearrange("p t c -> p (t c)"), acc[:, 2, :], ACT.Copy).then_inc(hi_done, 1)
            highs(0, 0, BC, True)
            act.wait_ge(cols_late_in, 7 * 16)

            def granule(G, first, last):
                for g in range(QUADS):
                    c = QUADS * G + g
                    if last and g == QUADS - 1:
                        continue
                    dd_rounded(c + 1, (g + 1) % 2, first and g == 0)
                    dd_full(c + 1, False)
                    highs(c + 1, (g + 1) % 2, AB, first and g == 0)
                    if g == 0 and not (first or last):
                        x_high(G + 1, False)
                    highs(c + 1, (g + 1) % 2, AC, first and g == 0)
                    if g == 0 and not (first or last):
                        square_high(G + 1)
                    if not first:
                        q_out(c, g % 2, False)
                    highs(c + 1, (g + 1) % 2, BC, first and g == 0)
                    if first and g == 0:
                        x_high(G + 1, False)
                        square_high(G + 1)
                    if first:
                        q_out(c, g % 2, g < 2)
                    if g == 0 and not last:
                        square_full(G + 1)

            over_granules(act, granule)
            for h in range(HALVES):
                act.wait_ge(half_done, h + 1)
                nc.scalar.activation(q_sb[0:UNITS, 1, h * BANK:(h + 1) * BANK], acc[UNITS:P, 2 + h, :],
                                     ACT.Identity, bias=cols[UNITS:P, 0:1]).then_inc(q_ready, 1)

        @block.vector
        def _(dve):
            def x_low(G):
                dve.wait_ge(x_hi_done, G + 1)
                nc.vector.tensor_tensor(parts[:, 1, :].bitcast(F32R), x_cols(G), parts[:, 0, :],
                                        ALU.subtract).then_inc(x_lo_done, 1)

            def sq_low(G):
                dve.wait_ge(sq_done, G + 1)
                nc.vector.tensor_tensor(parts[:, 3, :].bitcast(F32R), parts[:, 3, :], parts[:, 2, :],
                                        ALU.subtract).then_inc(sq_lo_done, 1)

            def sum_x(G):
                dve.wait_ge(x_in, 16 * G + 16)
                nc.vector.tensor_reduce(x_sum[:, bass.ds(G * BJ, BJ)], x_cols(G).rearrange("p (j d) -> p j d", d=EMB),
                                        AX_X, ALU.add).then_inc(x_summed, 1)

            def monomials(c, G, g, t, first, second=False):
                if t == AB and first:
                    dve.wait_ge(early_first_in, 32)
                    dve.wait_ge(early_rep_in, 32)
                    dve.wait_ge(early_b_in, 32)
                    dve.wait_ge(early_b_rest_in, 32)
                elif t == AB:
                    if second:
                        dve.wait_ge(second_rep_in, 16 * QUADS)
                    else:
                        dve.wait_ge(rep_in[g // 2], 16 * (QUADS - 1) * pairs_in(G, g // 2))
                    dve.wait_ge(b_in[g // 2], 16 * QUADS * (G + 1))
                if t == AC:
                    dve.wait_ge(c_rolled, c + 1)
                if not first:
                    dve.wait_ge(lo_ready, len(PRODUCTS) * (c - 1) + TURN[t])
                a, b = x_rep[:, g, :], b_rep[:, g, :]
                one, other = (a, b) if t == AB else (rolled[:, 0, :, :].rearrange("p a b -> p (a b)"), a if t == AC else b)
                nc.vector.tensor_tensor(z[:, t, :], one, other, ALU.mult).then_inc(z_done, 1)

            def square_low(c, s, first):
                dve.wait_ge(squared, c + 1)
                if not first:
                    dve.wait_ge(z_used, TILES * (c - 2) + DD + 1)
                nc.vector.tensor_tensor(z_lo[:, s, DD, :], z[:, DD, :], z_hi[:, s, DD, :].bitcast(F32),
                                        ALU.subtract).then_inc(square_lo_ready, 1)

            def final_low(c, s):
                dve.wait_ge(hi_ready, TILES * c + HI_TURN[AC])
                dve.wait_ge(z_used, TILES * (c - 2) + AC + 1)
                nc.vector.tensor_tensor(z_lo[:, s, AC, :], z[:, AC, :], z_hi[:, s, AC, :].bitcast(F32),
                                        ALU.subtract).then_inc(final_lo_ready, 1)

            def h_times_q(c, s, G, pair_slot, slot_taken):
                dve.wait_ge(q_ready, c + 1)
                if slot_taken:
                    dve.wait_ge(summed, 2 * G + pair_slot - 1)
                nc.vector.scalar_tensor_tensor(
                    out=hq[UNITS * s:UNITS * (s + 1), pair_slot, :],
                    in0=acc[0:UNITS, 2 * s:2 * s + 2, :].rearrange("p a b -> p (a b)"), scalar=cols[0:UNITS, 0:1],
                    in1=q_sb[0:UNITS, s, :], op0=ALU.add, op1=ALU.mult).then_inc(hq_done, 1)

            def sum_hq(G, pair_slot):
                dve.wait_ge(hq_done, QUADS * G + 2 * pair_slot + 2)
                nc.vector.tensor_reduce(hq_sum[:, pair_slot, bass.ds(G * BJ, BJ)],
                                        hq[:, pair_slot, :].rearrange("p (j d) -> p j d", d=EMB),
                                        AX_X, ALU.add).then_inc(summed, 1)

            nc.vector.memset(low[0:UNITS, 0:2, :], 0.0).then_inc(low_zero, 1)
            dve.wait_ge(rolls_read, 16)
            nc.vector.tensor_copy(rolls[:].rearrange("p t c -> p (t c)"), rolls_f).then_inc(rolls_ready, 1)
            x_low(0)
            sq_low(0)
            sum_x(0)
            dve.wait_ge(v_done, 1)
            nc.vector.tensor_copy(v_w2[:, 0:FIELDS], acc[0:UNITS, 0, 0:FIELDS]).then_inc(v_copied, 1)
            nc.vector.tensor_copy(v_rep[:], acc[0:UNITS, 0, 0:FIELDS].unsqueeze(1).to_broadcast((UNITS, QUADS, FIELDS))
                                  ).then_inc(v_copied, 1)
            monomials(0, 0, 0, AB, True)
            monomials(0, 0, 0, AC, True)
            dve.wait_ge(g_copied, 2)
            for k in range(2):
                nc.vector.tensor_copy(low[UNITS:P, k, :].rearrange("p (a b) -> p a b", a=G_BANKS),
                                      g_psum[:, :, :, FIELDS]).then_inc(low_done, 1)
            dve.wait_ge(w1_in, 16)
            nc.vector.tensor_copy(rows64(wg)[:, :, FIELDS:FIELDS + FIELDS // 2],
                                  rows64(wg)[:, :, 0:FIELDS // 2]).then_inc(wg_doubled, 1)
            nc.vector.tensor_copy(rows64(wgt)[:, :, 0:FIELDS],
                                  rows64(wg)[:, :, 0:FIELDS].rearrange("p r m -> p m r")).then_inc(wg_doubled, 1)
            dve.wait_ge(wg_doubled, 2)
            dve.wait_ge(wgt_done, 1)
            w_k, wt_k = diagonals(wg), diagonals(wgt)

            def both_orders(to, pick):
                nc.vector.tensor_tensor(to, pick(w_k), pick(wt_k), ALU.add).then_inc(sym_done, 1)

            both_orders(sym[:, DD, 0:2, :], lambda w: w[:, 12:14, :])
            both_orders(sym[:, DD, 2:3, :], lambda w: w[:, 15:16, :])
            nc.vector.tensor_copy(sym[:, DD, 3:4, :], w_k[:, 16:17, :]).then_inc(sym_done, 1)
            dve.wait_ge(table_in, 1)
            nc.vector.tensor_copy(low[:, 2:4, :], w_k[:, 0:1, :].to_broadcast((P, 2, FIELDS))).then_inc(low_done, 1)
            both_orders(sym[:, AB, :, :], lambda w: w[:, 1:5, :])
            both_orders(sym[:, AC, :, :].rearrange("p (a k) m -> p a k m", a=2),
                        lambda w: w[:, 6:16, :].rearrange("p (a k) m -> p a k m", a=2)[:, :, 0:4:3, :])
            for side in range(2):
                both_orders(sym_bc[:, :, FIELDS * side:FIELDS * (side + 1)], lambda w: w[:, BC0:BC1 + 1, :])
            dve.wait_ge(dd_turned, 1)
            nc.vector.tensor_copy(w_dd[:], acc[:, 1, 0:P]).then_inc(dd_copied, 1)
            dve.wait_ge(sym_done, 3 + 4)
            for j in range(QUADS):
                b = ROLLS[B][j]
                nc.vector.tensor_copy(sym[:, BC, j, :], sym_bc[:, ROLLS[C][j] - b - BC0, b:b + FIELDS]).then_inc(sym_done, 1)
            monomials(0, 0, 0, BC, True)
            dve.wait_ge(hi_done, 1)
            nc.vector.tensor_tensor(low_lo[:], acc[:, 3, 0:P], low_hi[:].bitcast(F32), ALU.subtract).then_inc(weights_ready, 1)
            dve.wait_ge(hi_done, 2)
            nc.vector.tensor_tensor(w_lo[:].rearrange("p t c -> p (t c)"), acc[:, 2, :],
                                    w_hi[:].bitcast(F32).rearrange("p t c -> p (t c)"), ALU.subtract).then_inc(weights_ready, 1)
            nc.vector.tensor_copy(beta[:], acc[:, 3, 2 * P:2 * P + 1]).then_inc(beta_ready, 1)
            square_low(0, 0, True)
            monomials(1, 0, 1, AB, False, second=True)
            dve.wait_ge(beta_ready, 1)
            dve.wait_ge(cols_late_in, 7 * 16)
            nc.vector.tensor_scalar(beta_pick[:], picks[:, 2, :], beta[:, 0:1], None, ALU.mult).then_inc(tail_ready, 1)
            nc.vector.tensor_copy(b23[:], cols[:, 3:4].to_broadcast((P, P))).then_inc(tail_ready, 1)
            nc.vector.tensor_scalar(w23[:], cols[:, 4:5].to_broadcast((P, QUADS)), float(EMB), None, ALU.mult).then_inc(tail_ready, 1)

            def granule(G, first, last):
                for g in range(QUADS):
                    c = QUADS * G + g
                    nG, ng = (G, g + 1) if g < QUADS - 1 else (G + 1, 0)
                    more = not (last and g == QUADS - 1)
                    if more and not (first and g == 0):
                        monomials(c + 1, nG, ng, AB, False)
                    if more:
                        monomials(c + 1, nG, ng, AC, False)
                    if not (first and g == 0):
                        h_times_q(c - 1, (g + 1) % 2, G if g else G - 1, ((g + 3) % 4) // 2, g % 2 == 1 and not first)
                    if more:
                        monomials(c + 1, nG, ng, BC, False)
                    if more:
                        if last and g == QUADS - 2:
                            final_low(c + 1, (g + 1) % 2)
                        square_low(c + 1, (g + 1) % 2, first and g == 0)
                    if g == (1 if first else 0) and not last:
                        x_low(G + 1)
                    if g == 1 and not last:
                        sq_low(G + 1)
                    if g == 0 and not first:
                        sum_hq(G - 1, 1)
                    if g == 3:
                        sum_hq(G, 0)
                    if g == (1 if last else 2) and not first:
                        sum_x(G)

            over_granules(dve, granule)
            for h in range(HALVES):
                cut = slice(h * BANK, (h + 1) * BANK)
                dve.wait_ge(q_ready, CHUNKS + h)
                if h == 0:
                    dve.wait_ge(summed, 2 * GRANULES - 1)
                nc.vector.scalar_tensor_tensor(
                    out=hq[UNITS:P, 1, cut], in0=acc[0:UNITS, 2 + h, :], scalar=cols[0:UNITS, 0:1],
                    in1=q_sb[0:UNITS, 1, cut], op0=ALU.add, op1=ALU.mult).then_inc(hq_done, 1)
                dve.wait_ge(hq_done, CHUNKS + h)
                at = (GRANULES - 1) * BJ + h * BJ // HALVES
                nc.vector.tensor_reduce(hq_sum[:, 1, at:at + BJ // HALVES], hq[:, 1, cut].rearrange("p (j d) -> p j d", d=EMB),
                                        AX_X, ALU.add).then_inc(summed, 1)
            dve.wait_ge(y_done, 1)
            nc.vector.tensor_scalar(y_sb[:], rolled[:, 1, 0, 0:QUADS], cols[:, 5:6], None, ALU.add).then_inc(y_ready, 1)

        @block.tensor
        def _(pe):
            pe.wait_ge(w3_in, 16)
            pe.wait_ge(w3_col_in, 16)
            w3_v = w3_sb.rearrange("p (h m) -> p m h", m=FIELDS)
            w2_v = w2_sb.rearrange("p (h m) -> p m h", m=FIELDS)
            for m in range(FIELDS):
                mm = nc.tensor.matmul(acc[0:UNITS, 0, m:m + 1], w3_v[:, m, :], w3_col[UNITS:P, :], start=True, stop=True)
            mm.then_inc(v_done, 1)

            def g_and_l(fields):
                for m in fields:
                    at = (m % G_FIELDS) * (FIELDS + 1)
                    mm = nc.tensor.matmul(acc[UNITS:P, m // G_FIELDS, at:at + FIELDS + 1], w2_v[:, m, :], v_w2[:],
                                          start=True, stop=True)
                return mm

            def roll(c, G, g, i, first):
                if i == D:
                    pe.wait_ge(stack_in[g], 16 * KINDS * (G + 1))
                if not first:
                    if i == C:
                        pe.wait_ge(z_done, len(PRODUCTS) * c)
                    else:
                        pe.wait_ge(squared, c)
                for h in range(HALVES):
                    mm = nc.tensor.matmul(rolled[:, i - C, h, :], rolls[:, i - C, :],
                                          stack[:, g, h * BANK:(h + 1) * BANK], start=True, stop=True)
                mm.then_inc(c_rolled if i == C else d_rolled, 1)

            pe.wait_ge(w2_in, 16)
            pe.wait_ge(w2_col_in, 16)
            pe.wait_ge(v_copied, 2)
            g_and_l(range(0, 16)).then_inc(g_done, 1)
            g_and_l(range(16, 24))
            pe.wait_ge(rolls_ready, 1)
            roll(0, 0, 0, D, True)
            g_and_l(range(24, 32)).then_inc(g_done, 1)
            roll(0, 0, 0, C, True)
            roll(1, 0, 1, D, False)
            pe.wait_ge(consts_in, 16)

            def turn(to, t):
                return nc.tensor.matmul(to, sym[:, t, :, :].rearrange("p k m -> p (k m)"), eye_half if t == DD else eye,
                                        start=True, stop=True)

            pe.wait_ge(sym_done, 3)
            turn(acc[:, 1, 0:P], DD).then_inc(dd_turned, 1)
            for t, ready in ((DD, 3), (AB, 4), (AC, 5)):
                pe.wait_ge(sym_done, ready)
                turn(acc[:, 2, t * P:(t + 1) * P], t)
            pe.wait_ge(low_zero, 1)
            pe.wait_ge(low_done, 3)
            pe.wait_ge(cols_late_in, 7 * 16)
            nc.tensor.matmul(acc[:, 3, 2 * P:2 * P + 1], v_rep[:].rearrange("p g m -> p (g m)"), cols[0:UNITS, 3:4],
                             start=True, stop=True)
            nc.tensor.matmul(acc[:, 3, 0:P], low[:].rearrange("p k m -> p (k m)"), eye, start=True, stop=False)
            pe.wait_ge(dd_copied, 1)
            nc.tensor.matmul(acc[:, 3, 0:P], excess, w_dd[:], start=False, stop=True).then_inc(low_turned, 1)
            pe.wait_ge(sym_done, 7 + QUADS)
            turn(acc[:, 2, BC * P:(BC + 1) * P], BC).then_inc(turned, 1)
            pe.wait_ge(weights_ready, 1)

            def lo_wait(c, t, final):
                if t == DD:
                    pe.wait_ge(square_lo_ready, c + 1)
                elif final and t == AC:
                    pe.wait_ge(final_lo_ready, 1)
                else:
                    pe.wait_ge(lo_ready, len(PRODUCTS) * c + TURN[t] - (final and t == BC))

            def granule(G, first, last):
                for g in range(QUADS):
                    c, s = QUADS * G + g, g % 2
                    nG, ng = (G, g + 1) if g < QUADS - 1 else (G + 1, 0)

                    def out(h):
                        return acc[:, 2 * s + h, :]

                    final = last and g == QUADS - 1
                    if not (final or first and g == 0):
                        roll(c + 1, nG, ng, D, False)
                    if not (first and g < 2):
                        pe.wait_ge(hq_done, c - 1)
                    for h in range(HALVES):
                        cut = stack[:, g, h * BANK:(h + 1) * BANK]
                        nc.tensor.matmul(out(h), low_hi[:], cut, start=True, stop=False)
                        mm = nc.tensor.matmul(out(h), low_lo[:], cut, start=False, stop=False)
                    mm.then_inc(stack_used, 1)
                    if first and g == 0:
                        pe.wait_ge(weights_ready, 2)
                        pe.wait_ge(beta_ready, 1)

                    def rounded(t, h):
                        cut = z_hi[:, s, t, h * BANK:(h + 1) * BANK]
                        nc.tensor.matmul(out(h), w_hi[:, t, :], cut, start=False, stop=False)
                        nc.tensor.matmul(out(h), w_lo[:, t, :], cut, start=False, stop=False)

                    def rest(t, h):
                        return nc.tensor.matmul(out(h), w_hi[:, t, :], z_lo[:, s, t, h * BANK:(h + 1) * BANK],
                                                start=False, stop=t == TILES - 1)

                    for t in range(TILES):
                        if t == AC and not final:
                            roll(c + 1, nG, ng, C, False)
                        pe.wait_ge(hi_ready, TILES * c + HI_TURN[t])
                        if final and t == TILES - 1:
                            for h in range(HALVES):
                                rounded(t, h)
                                if h == 0:
                                    lo_wait(c, t, final)
                                rest(t, h).then_inc(half_done, 1)
                            continue
                        for h in range(HALVES):
                            rounded(t, h)
                        lo_wait(c, t, final)
                        for h in range(HALVES):
                            mm = rest(t, h)
                        mm.then_inc(z_used, 1)

            over_granules(pe, granule)
            pe.wait_ge(tail_ready, 3)
            pe.wait_ge(x_summed, GRANULES)
            out = rolled[:, 1, 0, 0:QUADS]
            nc.tensor.matmul(out, b23[:], w23[:], start=True, stop=False)
            nc.tensor.matmul(out, x_sum[:], beta_pick[:], start=False, stop=False)
            pe.wait_ge(summed, 2 * GRANULES - 1)
            nc.tensor.matmul(out, hq_sum[:, 0, :], picks[:, 0, :], start=False, stop=False)
            pe.wait_ge(summed, 2 * GRANULES + 1)
            nc.tensor.matmul(out, hq_sum[:, 1, :], picks[:, 1, :], start=False, stop=True).then_inc(y_done, 1)


def kernel(r_x0, L0_rec_W1, L0_rec_b1, L0_rec_W2, L0_rec_b2, L0_rec_W3, L0_rec_b3, L0_rec_W_out, L0_rec_b_out):
    import concourse.bacc as bacc
    from concourse.bass_utils import run_bass_kernel_spmd

    names = ["x", "W1", "b1", "W2", "b2", "W3", "b3", "W_out", "b_out"]
    given = [r_x0, L0_rec_W1, L0_rec_b1, L0_rec_W2, L0_rec_b2, L0_rec_W3, L0_rec_b3, L0_rec_W_out, L0_rec_b_out]
    arrays = {n: np.ascontiguousarray(a) for n, a in zip(names, given)}
    arrays["turns_in"], arrays["rolls_in"], arrays["picks_in"] = constants()

    nc = bacc.Bacc("TRN2", target_bir_lowering=False, num_devices=1)
    args = [nc.dram_tensor(n, a.shape, mybir.dt.from_np(a.dtype), kind="ExternalInput").ap() for n, a in arrays.items()]
    y = nc.dram_tensor("y", (arrays["x"].shape[0], 1), F32, kind="ExternalOutput").ap()
    build(nc, *args, y)
    result = run_bass_kernel_spmd(nc, [arrays], core_ids=[0])
    return result.results[0]["y"]
```
